# Optimizing a Trainium2 kernel written in Bass

```python
import numpy as np
import jax
import jax.numpy as jnp

def _softmax(x, axis=-1):
    return jax.nn.softmax(x, axis=axis)

def _gelu(x):
    return jax.nn.gelu(x, approximate=True)

def _silu(x):
    return jax.nn.silu(x)

def _sigmoid(x):
    return jax.nn.sigmoid(x)

def _layernorm(x, axis=-1, eps=1e-05):
    m = jnp.mean(x, axis=axis, keepdims=True)
    v = jnp.var(x, axis=axis, keepdims=True)
    return (x - m) / jnp.sqrt(v + eps)

def _scatter_add(tgt, idx, src, axis=0):
    return tgt.at[idx].add(src)

def _segment_sum(src, seg, n):
    return jax.ops.segment_sum(src, seg, n)
kernel_name = 'mk_macaron_d1_jaxref_r8_444efa'

def setup_inputs(seed: int=0):
    np.random.seed(seed)
    _w = jnp.asarray

    def _L0_attn_setup():
        import jax, jax.numpy as jnp
        import numpy as np
        B, N, D = (1, 256, 128)
        H = 16
        HD = D // H
        MAX_REL = 100
        NUM_EMB = 2 * MAX_REL - 1
        NEG = 100000000.0

        def _rel_pos_logits(q_pos, rel_emb):
            L = q_pos.shape[0]
            pad_len = max(L - MAX_REL, 0)
            start = max(MAX_REL - L, 0)
            padded = jnp.pad(rel_emb, ((0, 0), (pad_len, pad_len), (0, 0)))
            used = padded[:, start:start + 2 * L - 1, :]
            q4 = q_pos.reshape(L, -1, H, HD)
            logits = jnp.einsum('lbhd,hmd->lbhm', q4, used)
            logits = logits.reshape(L, -1, 2 * L - 1)
            if pad_len > 0:
                logits = logits.at[:, :, :pad_len].add(-NEG)
                logits = logits.at[:, :, -pad_len:].add(-NEG)
            bh = logits.shape[1]
            x = jnp.pad(logits, ((0, 0), (0, 0), (0, 1)))
            x = jnp.transpose(x, (1, 0, 2)).reshape(bh, L * 2 * L)
            x = jnp.pad(x, ((0, 0), (0, L - 1)))
            x = x.reshape(bh, L + 1, 2 * L - 1)
            return x[:, :L, L - 1:]
        key = jax.random.key(seed)
        ks = jax.random.split(key, 6)
        x = jax.random.normal(ks[0], (B, N, D), dtype=jnp.float32)
        qkv_w = jax.random.normal(ks[1], (3 * D, D), dtype=jnp.float32) * 0.02
        qkv_b = jnp.zeros((3 * D,), dtype=jnp.float32)
        proj_w = jax.random.normal(ks[2], (D, D), dtype=jnp.float32) * 0.02
        proj_b = jnp.zeros((D,), dtype=jnp.float32)
        rel_emb = jax.random.normal(ks[3], (H, NUM_EMB, HD), dtype=jnp.float32) * HD ** (-0.5)
        return {'x': x, 'qkv_w': qkv_w, 'qkv_b': qkv_b, 'proj_w': proj_w, 'proj_b': proj_b, 'rel_emb': rel_emb}
    _L0_attn_in = _L0_attn_setup()

    def _L0_ffn_setup():
        import jax, jax.numpy as jnp
        import numpy as np
        DIM = 128
        HIDDEN = 512
        E = 8
        K = 2

        def _ffn_hidden(h, multiple_of=32):
            h = int(2 * h / 3)
            return multiple_of * ((h + multiple_of - 1) // multiple_of)
        EXP_HID = _ffn_hidden(HIDDEN)
        SH_HID = _ffn_hidden(HIDDEN // 2)

        def _swiglu(t, a, b, c):
            return jax.nn.silu(t @ a) * (t @ c) @ b
        key = jax.random.key(seed)
        ks = jax.random.split(key, 8)

        def xavier(k, shape, fan_in, fan_out):
            lim = np.sqrt(6.0 / (fan_in + fan_out)).astype(np.float32)
            return jax.random.uniform(k, shape, jnp.float32, -lim, lim)
        return {'x': jax.random.normal(ks[0], (2, 256, DIM), jnp.float32), 'gate_w': xavier(ks[1], (E, DIM), DIM, E), 'w1': xavier(ks[2], (E, DIM, EXP_HID), DIM, EXP_HID), 'w2': xavier(ks[3], (E, EXP_HID, DIM), EXP_HID, DIM), 'w3': xavier(ks[4], (E, DIM, EXP_HID), DIM, EXP_HID), 'sw1': xavier(ks[5], (DIM, SH_HID), DIM, SH_HID), 'sw2': xavier(ks[6], (SH_HID, DIM), SH_HID, DIM), 'sw3': xavier(ks[7], (DIM, SH_HID), DIM, SH_HID)}
    _L0_ffn_in = _L0_ffn_setup()
    _d = {'L0_attn_x': _L0_attn_in['x'], 'L0_attn_qkv_w': _L0_attn_in['qkv_w'], 'L0_attn_qkv_b': _L0_attn_in['qkv_b'], 'L0_attn_proj_w': _L0_attn_in['proj_w'], 'L0_attn_proj_b': _L0_attn_in['proj_b'], 'L0_attn_rel_emb': _L0_attn_in['rel_emb'], 'L0_ffn_gate_w': _L0_ffn_in['gate_w'], 'L0_ffn_w1': _L0_ffn_in['w1'], 'L0_ffn_w2': _L0_ffn_in['w2'], 'L0_ffn_w3': _L0_ffn_in['w3'], 'L0_ffn_sw1': _L0_ffn_in['sw1'], 'L0_ffn_sw2': _L0_ffn_in['sw2'], 'L0_ffn_sw3': _L0_ffn_in['sw3']}
    _x0 = _d['L0_attn_x']
    _d['L0_attn_x'] = jax.random.normal(jax.random.fold_in(jax.random.key(seed), 1), (4, 512, 128), dtype=_x0.dtype)
    del _x0
    return _d

def reference(L0_attn_x, L0_attn_qkv_w, L0_attn_qkv_b, L0_attn_proj_w, L0_attn_proj_b, L0_attn_rel_emb, L0_ffn_gate_w, L0_ffn_w1, L0_ffn_w2, L0_ffn_w3, L0_ffn_sw1, L0_ffn_sw2, L0_ffn_sw3):

    def _L0_attn_ref(x, qkv_w, qkv_b, proj_w, proj_b, rel_emb):
        import jax, jax.numpy as jnp
        import numpy as np
        B, N, D = (1, 256, 128)
        H = 16
        HD = D // H
        MAX_REL = 100
        NUM_EMB = 2 * MAX_REL - 1
        NEG = 100000000.0

        def _rel_pos_logits(q_pos, rel_emb):
            L = q_pos.shape[0]
            pad_len = max(L - MAX_REL, 0)
            start = max(MAX_REL - L, 0)
            padded = jnp.pad(rel_emb, ((0, 0), (pad_len, pad_len), (0, 0)))
            used = padded[:, start:start + 2 * L - 1, :]
            q4 = q_pos.reshape(L, -1, H, HD)
            logits = jnp.einsum('lbhd,hmd->lbhm', q4, used)
            logits = logits.reshape(L, -1, 2 * L - 1)
            if pad_len > 0:
                logits = logits.at[:, :, :pad_len].add(-NEG)
                logits = logits.at[:, :, -pad_len:].add(-NEG)
            bh = logits.shape[1]
            x = jnp.pad(logits, ((0, 0), (0, 0), (0, 1)))
            x = jnp.transpose(x, (1, 0, 2)).reshape(bh, L * 2 * L)
            x = jnp.pad(x, ((0, 0), (0, L - 1)))
            x = x.reshape(bh, L + 1, 2 * L - 1)
            return x[:, :L, L - 1:]
        b, n, d = x.shape
        qkv = x @ qkv_w.T + qkv_b
        qkv = qkv.reshape(b, n, 3, H, HD).transpose(2, 0, 3, 1, 4)
        q, k, v = (qkv[0], qkv[1], qkv[2])
        scale = 1.0 / np.sqrt(HD).astype(np.float32)
        logits = jnp.einsum('bhqd,bhkd->bhqk', q, k) * scale
        q_pos = jnp.transpose(q, (0, 2, 1, 3)).reshape(n, b * H, HD)
        pos = _rel_pos_logits(q_pos, rel_emb).reshape(b, H, n, n)
        probs = jax.nn.softmax(logits + pos, axis=-1)
        out = jnp.einsum('bhqk,bhkd->bhqd', probs, v)
        out = jnp.transpose(out, (0, 2, 1, 3)).reshape(b, n, d)
        return out @ proj_w.T + proj_b

    def _L0_ffn_ref(x, gate_w, w1, w2, w3, sw1, sw2, sw3):
        import jax, jax.numpy as jnp
        import numpy as np
        DIM = 128
        HIDDEN = 512
        E = 8
        K = 2

        def _ffn_hidden(h, multiple_of=32):
            h = int(2 * h / 3)
            return multiple_of * ((h + multiple_of - 1) // multiple_of)
        EXP_HID = _ffn_hidden(HIDDEN)
        SH_HID = _ffn_hidden(HIDDEN // 2)

        def _swiglu(t, a, b, c):
            return jax.nn.silu(t @ a) * (t @ c) @ b
        B, S, D = x.shape
        xt = x.reshape(-1, D)
        T = xt.shape[0]
        logits = xt @ gate_w.T
        scores = jax.nn.softmax(logits, axis=-1)
        topk_w, topk_i = jax.lax.top_k(scores, K)
        comb = jnp.zeros((T, E), x.dtype).at[jnp.arange(T)[:, None], topk_i].add(topk_w)
        y = jnp.zeros_like(xt)
        for e in range(E):
            y = y + comb[:, e:e + 1] * _swiglu(xt, w1[e], w2[e], w3[e])
        y = y.reshape(B, S, D)
        return y + _swiglu(x, sw1, sw2, sw3)
    x = L0_attn_x
    x = x + 0.5 * _L0_ffn_ref(_layernorm(x, axis=-1), L0_ffn_gate_w, L0_ffn_w1, L0_ffn_w2, L0_ffn_w3, L0_ffn_sw1, L0_ffn_sw2, L0_ffn_sw3)
    x = x + _L0_attn_ref(_layernorm(x, axis=-1), L0_attn_qkv_w, L0_attn_qkv_b, L0_attn_proj_w, L0_attn_proj_b, L0_attn_rel_emb)
    x = x + 0.5 * _L0_ffn_ref(_layernorm(x, axis=-1), L0_ffn_gate_w, L0_ffn_w1, L0_ffn_w2, L0_ffn_w3, L0_ffn_sw1, L0_ffn_sw2, L0_ffn_sw3)
    return x

_drawn_inputs = setup_inputs


def setup_inputs(seed=0):
    import zlib

    import numpy as np

    out = dict(_drawn_inputs(seed))
    spreads = {'L0_attn_qkv_b': (0.0, 0.316), 'L0_attn_proj_b': (0.0, 0.1)}
    factors = {'L0_attn_qkv_w': 8.0, 'L0_attn_rel_emb': 8.0}
    for name, (base, spread) in spreads.items():
        noise = np.random.default_rng([zlib.crc32(name.encode()), seed]).standard_normal(out[name].shape)
        drawn = base * np.exp(spread * noise) if base else spread * noise
        out[name] = jnp.asarray(drawn.astype(out[name].dtype))
    for name, factor in factors.items():
        out[name] = (out[name] * factor).astype(out[name].dtype)
    return out
```

```python
from contextlib import ExitStack

import concourse.bass as bass
from concourse import mybir

ALU = mybir.AluOpType
ACT = mybir.ActivationFunctionType
AX = mybir.AxisListType.X
F32 = mybir.dt.float32
F32R = mybir.dt.float32r
BF16 = mybir.dt.bfloat16

P = 128
B, N, D = 4, 512, 128
NT = N // P
E, EH, SH = 8, 352, 192
EPS = 1e-5
H, HD = 16, 8
NJ = H // 4
REACH = 99
NREL = 2 * REACH + 1
RW = NREL + 1
WIN = P + 2 * (REACH + 1)
OFF = P - (REACH + 1)
NEG = -1e8
QW = 232
QL = 32
QP = QL + NREL + QL + 1
ROW = H * QP
QS = P * (ROW + 1)
SCALE = float(1.0 / (8.0 ** 0.5))


def chunks(width):
    return [(c, min(P, width - c)) for c in range(0, width, P)]


EC, SC = chunks(EH), chunks(SH)
XC = [SC] + [EC] * E
UNITS = [(x, c) for x in range(E + 1) for c in range(len(XC[x]))]
NU = len(UNITS)
QT_CHUNKS = [[t for t in (qt - 1, qt, qt + 1) if 0 <= t < NT] for qt in range(NT)]


def head_steps():
    steps = []
    for n in range(NT * H + H):
        if n < NT * H:
            steps += [("dot", n), ("score", n)]
        if 0 <= n - 2 < NT * H:
            steps += [("turn", n - 2), ("exp", n - 2)]
        m = n - 3
        if 0 <= m < NT * H:
            steps.append(("pv", m))
            if m % H == H - 1:
                steps.append(("norm", m // H))
        if m >= H and m % H == 1:
            steps.append(("oT", m // H - 1))
        if m >= H and m % H == 3:
            steps += [("proj", m // H - 1), ("add", m // H - 1)]
    return steps


STEPS = head_steps()
TURNED = [s for s in STEPS if s[0] in ("turn", "oT", "proj")]


def slot(kind, n):
    return 4 + TURNED.index((kind, n)) % 3


class Count:

    def __init__(self, sem, *pers):
        self.sem, self.pers = sem, pers

    def wait_before(self, eng, b):
        k, turn = b
        eng.wait_ge(self.sem, turn * self.pers[k] + B * sum(self.pers[:k]))

    def wait(self, eng, b, n):
        k, turn = b
        eng.wait_ge(self.sem, turn * self.pers[k] + (B * sum(self.pers[:k]) + n))


def macaron_kernel(nc, x_d, gate_d, w1_d, w2_d, w3_d, sw1_d, sw2_d, sw3_d, wq_d, wk_d, wv_d, bq_d, bk_d, bv_d,
                   wp_d, bp_d, rel_d, ident_d, part_d, tri_d, out_d, scratch, qk_d, v_d):
    with ExitStack() as ctx:
        def sb(name, shape, dt=F32):
            return ctx.enter_context(nc.sbuf_tensor(name, shape, dt))

        def count(name, *pers):
            return Count(ctx.enter_context(nc.semaphore(name)), *pers)

        def sem(name):
            return ctx.enter_context(nc.semaphore(name))

        bank = ctx.enter_context(nc.psum_tensor("bank", [P, 8, 512], F32))

        w1 = sb("w1", [P, E, EH]); w3 = sb("w3", [P, E, EH]); w2 = sb("w2", [P, E, len(EC), D])
        sw1 = sb("sw1", [P, SH]); sw3 = sb("sw3", [P, SH]); sw2 = sb("sw2", [P, len(SC), D])
        gate = sb("gate", [P, E])
        wq = sb("wq", [P, NJ, P]); wk = sb("wk", [P, NJ, P]); wv = sb("wv", [P, D]); wp = sb("wp", [P, D])
        bq = sb("bq", [P, NJ]); bk = sb("bk", [P, NJ]); bks = sb("bks", [P, NJ]); bv = sb("bv", [P, D]); bp = sb("bp", [P, D])
        part = sb("part", [P, 6])
        rel = sb("rel", [P, NJ, RW]); rel_hi = sb("rel_hi", [P, NJ, RW], F32R); relr = sb("relr", [P, NJ, RW], F32R)
        ident = sb("ident", [P, P]); ident_b = sb("ident_b", [P, P], BF16); ones_b = sb("ones_b", [P, P], BF16)
        tri = sb("tri", [P, E, E])
        mhalf = sb("mhalf", [P, NT])
        x = sb("x", [P, B * NT, D])
        stats = sb("stats", [P, NT, 6]); mv = sb("mv", [P, NT, 2]); ve = sb("ve", [P, NT]); rstd = sb("rstd", [P, NT])
        xn = sb("xn", [P, NT, D]); xnT = sb("xnT", [P, N])
        gmax = sb("gmax", [P, NT]); gl = sb("gl", [P, NT, E]); gp = sb("gp", [P, NT, E]); gsum = sb("gsum", [P, NT])
        ginv = sb("ginv", [P, NT]); above = sb("above", [P, NT, E, E]); level = sb("level", [P, NT, E, E])
        rank = sb("rank", [P, NT, E]); comb = sb("comb", [P, NT, E])
        th = sb("th", [P, 2, N]); hs = sb("hs", [P, 2, N]); gT = sb("gT", [P, 2, len(EC), N]); acc = sb("acc", [P, NT, D])
        hi = sb("hi", [P, 2, N], F32R); lo = sb("lo", [P, 2, N])
        qk = sb("qk", [P, 2 * NJ, N], F32R); v = sb("v", [P, NT, H, HD + 1])
        rl = sb("rl", [P, 2, 4, 2, QP])
        skew = sb("skew", [P, 2, H, WIN])
        sc = sb("sc", [P, 3, 3 * P]); smax = sb("smax", [P, 4]); shift = sb("shift", [P, 2, P], BF16)
        pT = sb("pT", [P, 2, 3 * P])
        orec = sb("orec", [P, H]); on = sb("on", [P, 2, H, HD]); onT = sb("onT", [P, 2, P]); xb = sb("xb", [P, NT, D])

        s_w = sem("s_w"); s_wffn = sem("s_wffn"); s_x = sem("s_x"); s_cst = sem("s_cst"); s_rel = sem("s_rel")
        paced = sem("paced")
        s_stats = count("s_stats", 2 * NT, NT); s_mv = count("s_mv", 2 * NT, NT); s_ve = count("s_ve", 2, 1)
        s_rstd = count("s_rstd", 2, 1); s_xn = count("s_xn", 2, 1); s_tr = count("s_tr", 2, 1); s_xnT = count("s_xnT", 2, 1)
        s_gate = count("s_gate", 1, 1); s_gl = count("s_gl", 2, 2); s_gp = count("s_gp", 1, 1); s_gv = count("s_gv", 8, 8)
        s_comb = count("s_comb", 1, 1)
        s_h = count("s_h", NU, NU); s_th = count("s_th", NU, NU); s_hs = count("s_hs", NU, NU); s_g = count("s_g", NU, NU)
        s_y = count("s_y", E + 1, E + 1); s_acc = count("s_acc", E + 1, E + 1)
        s_v = count("s_v", 1); s_vb = count("s_vb", 1)
        s_p = count("s_p", 2 * NJ); s_hi = count("s_hi", 2 * NJ); s_lo = count("s_lo", 2 * NJ); s_qk = count("s_qk", 2 * NJ)
        NR = 2 * NJ
        s_r = count("s_r", NR); s_rl = [count(f"s_rl{i}", NR // 2) for i in range(2)]
        s_rw = [count(f"s_rw{i}", 32 * NR // 2, 0) for i in range(2)]
        s_qkvw = count("s_qkvw", 32, 0)
        s_tile = [count(f"s_tile{i}", 0, 32) for i in range(NT)]
        s_sk = [count(f"s_sk{i}", 0, 64 * NT // 2) for i in range(2)]
        NH = NT * H
        s_s = count("s_s", 0, NH); s_sc = count("s_sc", 0, NH); s_shift = count("s_shift", 0, NH); s_t = count("s_t", 0, NH)
        s_pT = count("s_pT", 0, NH); s_pv = count("s_pv", 0, NH); s_orec = count("s_orec", 0, NT); s_on = count("s_on", 0, NT)
        s_xb = count("s_xb", 0, NT); s_ot = count("s_ot", 0, NT); s_onT = count("s_onT", 0, NT); s_y2 = count("s_y2", 0, NT)
        s_x2 = count("s_x2", 0, NT); s_out = sem("s_out")

        block = ctx.enter_context(nc.Block())

        def hold(eng):
            eng.sem_inc(paced, 1)

        def xt(b, t):
            return x[:, bass.ds(b[1] * NT + t, 1), :].rearrange("p a d -> p (a d)")

        def scores_window(qt):
            return (REACH + 1 if qt == 0 else 0), (WIN - (REACH + 1) if qt == NT - 1 else WIN)


        @block.sync
        def _(sp):
            sp.dma_start(x[:], x_d.rearrange("b (t p) d -> p (b t) d", p=P)).then_inc(s_x, 16)
            for dst, src in ((ident, ident_d), (gate, gate_d), (tri, tri_d)):
                sp.dma_start(dst[:], src).then_inc(s_w, 16)
            sp.dma_start(sw1[:], sw1_d).then_inc(s_wffn, 16)
            sp.dma_start(sw3[:], sw3_d).then_inc(s_wffn, 16)
            for c, (r, m) in enumerate(SC):
                sp.dma_start(sw2[0:m, c, :], sw2_d[r:r + m, :]).then_inc(s_wffn, 16)
            sp.dma_start(w1[:], w1_d.rearrange("e d h -> d e h")).then_inc(s_wffn, 16)
            sp.dma_start(w3[:], w3_d.rearrange("e d h -> d e h")).then_inc(s_wffn, 16)
            for c, (r, m) in enumerate(EC):
                sp.dma_start(w2[0:m, :, c, :], w2_d[:, r:r + m, :].rearrange("e p d -> p e d")).then_inc(s_wffn, 16)
            for dst, src in ((wq, wq_d), (wk, wk_d), (wv, wv_d), (wp, wp_d), (bq, bq_d), (bk, bk_d), (bv, bv_d), (bp, bp_d),
                             (part, part_d), (rel, rel_d)):
                sp.dma_start(dst[:], src).then_inc(s_w, 16)
            with sp.Fori(0, B) as turn:
                b = (0, turn)
                s_vb.wait(sp, b, 1)
                hold(sp)
                s_qk.wait(sp, b, 2 * NJ)
                hold(sp)
                sp.dma_start(qk_d[bass.ds(turn, 1)].rearrange("a p f -> (a p) f"),
                             qk[:].bitcast(F32).rearrange("p j n -> p (j n)")).then_inc(s_qkvw.sem, 16)
                sp.dma_start(v_d[bass.ds(turn, 1)].rearrange("a p f -> (a p) f"),
                             v[:].rearrange("p t h d -> p (t h d)")).then_inc(s_qkvw.sem, 16)
                for n in range(NR):
                    pair, j = divmod(n, NJ)
                    s_rl[n % 2].wait(sp, b, n // 2 + 1)
                    hold(sp)
                    for i in range(2):
                        dst = bass.AP(scratch.tensor, scratch.offset + turn * QS + ((2 * pair + i) * NT * QS + 4 * j * QP),
                                      [[ROW + 1, P], [QP, 4], [1, QP - 1]])
                        sp.dma_start(dst, rl[:, n % 2, :, i, 0:QP - 1]).then_inc(s_rw[n % 2].sem, 16)
            for i in range(2):
                sp.wait_ge(s_rw[i].sem, B * s_rw[i].pers[0])
            sp.wait_ge(s_qkvw.sem, B * 32)
            with sp.Fori(0, B) as turn:
                b = (1, turn)

                def load_tile(turn, t):
                    sp.dma_start(qk[:, :, t * P:(t + 1) * P].bitcast(F32),
                                 qk_d[bass.ds(turn, 1)].rearrange("a p (j n) -> (a p) j n", n=N)[:, :, t * P:(t + 1) * P])\
                        .then_inc(s_tile[t].sem, 16)
                    sp.dma_start(v[:, t].rearrange("p h d -> p (h d)"),
                                 v_d[bass.ds(turn, 1)].rearrange("a p (t f) -> (a p) t f", t=NT)[:, t, :])\
                        .then_inc(s_tile[t].sem, 16)

                s_tr.wait_before(sp, b)
                hold(sp)
                for qt in range(NT):
                    if qt == 0:
                        for t in range(NT):
                            load_tile(turn, t)
                    if qt >= 2:
                        s_sc.wait(sp, b, (qt - 1) * H)
                        hold(sp)
                    for a in range(4):
                        src = bass.AP(scratch.tensor, scratch.offset + turn * (NT * QS) + (qt * QS + 32 * a * (ROW + 1) + QL - 1),
                                      [[ROW, 32], [QP, H], [1, QW]])
                        sp.dma_start(skew[32 * a:32 * a + 32, qt % 2, :, 32 * a:32 * a + QW], src).then_inc(s_sk[qt % 2].sem, 16)

            sp.wait_ge(s_out, 16 * B)

        @block.gpsimd
        def _(pool):
            nc.gpsimd.memset(skew[:], NEG).then_inc(s_cst, 1)
            nc.gpsimd.memset(rl[:], NEG).then_inc(s_cst, 1)
            nc.gpsimd.memset(mhalf[:], -0.5).then_inc(s_cst, 1)
            nc.gpsimd.memset(ones_b[:], 1.0).then_inc(s_cst, 1)
            nc.gpsimd.memset(v[:], 1.0).then_inc(s_cst, 1)
            nc.gpsimd.memset(sc[:], NEG).then_inc(s_cst, 1)
            pool.wait_ge(s_w, 16 * 13)
            nc.gpsimd.tensor_copy(ident_b[:], ident[:]).then_inc(s_cst, 1)
            pool.wait_ge(s_cst, 7)

            def rsqrt(b, l):
                s_ve.wait(pool, b, l + 1)
                nc.gpsimd.tensor_tensor(rstd[:], ve[:], mhalf[:], ALU.pow).then_inc(s_rstd.sem, 1)

            with pool.Fori(0, B) as turn:
                b = (0, turn)
                rsqrt(b, 0)
                rsqrt(b, 1)
            with pool.Fori(0, B) as turn:
                b = (1, turn)
                for n in range(NH):
                    s_sc.wait(pool, b, n + 1)
                    hold(pool)
                    if n >= 2:
                        s_t.wait(pool, b, n - 1)
                        hold(pool)
                    nc.gpsimd.tensor_scalar(shift[:, n % 2, :], ident[:], smax[:, n % 4:n % 4 + 1], -1.0,
                                            ALU.mult, ALU.mult).then_inc(s_shift.sem, 1)
                rsqrt(b, 0)

        @block.vector
        def _(dve):
            dve.wait_ge(s_w, 16 * 13)
            dve.wait_ge(s_x, 16)
            nc.vector.tensor_copy(rel_hi[:], rel[:]).then_inc(s_rel, 1)
            nc.vector.tensor_scalar(bks[:], bk[:], SCALE, None, ALU.mult).then_inc(s_rel, 1)
            dve.wait_ge(s_rel, 1)
            fl = "p j r -> p (j r)"
            nc.vector.tensor_scalar(rel[:], rel[:], part[:, 4:5], None, ALU.mult).then_inc(s_rel, 1)
            dve.wait_ge(s_rel, 3)
            nc.vector.scalar_tensor_tensor(relr[:].rearrange(fl), rel_hi[:].bitcast(F32).rearrange(fl), part[:, 3:4],
                                           rel[:].rearrange(fl), ALU.mult, ALU.add).then_inc(s_rel, 1)
            dve.wait_ge(s_cst, 7)
            def layernorm(b, l):
                if l == 1:
                    s_acc.wait(dve, b, E + 1)
                    hold(dve)
                if b[0] == 1:
                    s_x2.wait(dve, b, NT)
                    hold(dve)
                for t in range(NT):
                    nc.vector.bn_stats(stats[:, t, :], xt(b, t)).then_inc(s_stats.sem, 1)
                s_stats.wait(dve, b, l * NT + NT)
                hold(dve)
                for t in range(NT):
                    nc.vector.bn_aggr(mv[:, t, :], stats[:, t, :]).then_inc(s_mv.sem, 1)
                s_mv.wait(dve, b, l * NT + NT)
                nc.vector.tensor_scalar(ve[:], mv[:, :, 1], EPS, None, ALU.add).then_inc(s_ve.sem, 1)
                s_rstd.wait(dve, b, l + 1)
                hold(dve)
                for t in range(NT):
                    ins = nc.vector.tensor_scalar(xn[:, t, :], xt(b, t), mv[:, t, 0:1],
                                                  rstd[:, t:t + 1], ALU.subtract, ALU.mult)
                ins.then_inc(s_xn.sem, 1)

            def gating(b):
                def step(ins, n):
                    ins.then_inc(s_gv.sem, 1)
                    s_gv.wait(dve, b, n)

                logits = bank[:, 7, 0:NT * E].rearrange("p (t e) -> p t e", e=E)
                s_gate.wait(dve, b, 1)
                nc.vector.tensor_reduce(gmax[:], logits, AX, ALU.max).then_inc(s_gl.sem, 1)
                s_gl.wait(dve, b, 1)
                nc.vector.tensor_tensor(gl[:], logits, gmax[:].unsqueeze(2).broadcast_to([P, NT, E]),
                                        ALU.subtract).then_inc(s_gl.sem, 1)
                s_gp.wait(dve, b, 1)
                other = gp[:].unsqueeze(2).broadcast_to([P, NT, E, E])
                own = gp[:].unsqueeze(3).broadcast_to([P, NT, E, E])
                step(nc.vector.tensor_tensor(above[:], other, own, ALU.is_gt), 1)
                step(nc.vector.tensor_tensor(level[:], other, own, ALU.is_ge), 2)
                step(nc.vector.tensor_tensor(level[:], level[:], tri[:].unsqueeze(1).broadcast_to([P, NT, E, E]),
                                             ALU.mult), 3)
                step(nc.vector.tensor_tensor(above[:], above[:], level[:], ALU.max), 4)
                nc.vector.tensor_reduce(rank[:], above[:], AX, ALU.add).then_inc(s_gv.sem, 1)
                nc.vector.tensor_reduce(gsum[:], gp[:], AX, ALU.add).then_inc(s_gv.sem, 1)
                s_gv.wait(dve, b, 6)
                nc.vector.reciprocal(ginv[:], gsum[:]).then_inc(s_gv.sem, 1)
                nc.vector.scalar_tensor_tensor(comb[:], rank[:], 1.5, gp[:], ALU.is_lt, ALU.mult).then_inc(s_gv.sem, 1)
                s_gv.wait(dve, b, 8)
                nc.vector.scalar_tensor_tensor(comb[:], comb[:], 0.25, ginv[:].unsqueeze(2).broadcast_to([P, NT, E]),
                                               ALU.mult, ALU.mult).then_inc(s_comb.sem, 1)

            def hidden(b, u):
                xi, c = UNITS[u]
                m = XC[xi][c][1]
                n = u
                s_th.wait(dve, b, n + 1)
                nc.vector.scalar_tensor_tensor(hs[0:m, u % 2, :], th[0:m, u % 2, :], 1.0, bank[0:m, u % 2, :],
                                               ALU.add, ALU.mult).then_inc(s_hs.sem, 1)
                s_hs.wait(dve, b, n + 1)
                nc.vector.tensor_tensor(gT[0:m, xi % 2, c, :], hs[0:m, u % 2, :], bank[0:m, 2 + u % 2, :],
                                        ALU.mult).then_inc(s_g.sem, 1)

            def gather(b, xi):
                n = xi
                s_y.wait(dve, b, n + 1)
                hold(dve)
                if xi == 1:
                    s_comb.wait(dve, b, 1)
                    hold(dve)
                if xi:
                    s_acc.wait(dve, b, n)
                    hold(dve)
                for t in range(NT):
                    w = comb[:, t, xi - 1:xi] if xi else 0.25
                    before = acc[:, t, :] if xi else xt(b, t)
                    after = acc[:, t, :] if xi < E else xt(b, t)
                    ins = nc.vector.scalar_tensor_tensor(after, bank[:, 4 + xi % 2, t * D:(t + 1) * D], w, before,
                                                         ALU.mult, ALU.add)
                ins.then_inc(s_acc.sem, 1)

            def ffn(b):
                layernorm(b, 0)
                gating(b)
                u = 0
                for xi in range(E + 1):
                    for c in range(len(XC[xi])):
                        hidden(b, u)
                        u += 1
                    if xi:
                        gather(b, xi - 1)
                gather(b, E)

            def split(b, i):
                wide = bank[:, 4 + i % 2, :]
                bias = (bq if i < NJ else bk)[:, i % NJ:i % NJ + 1]
                s_hi.wait(dve, b, i + 1)
                whole = part[:, 2:3] if i < NJ else part[:, 5:6]
                nc.vector.tensor_scalar(lo[:, i % 2, :], wide, bias, whole, ALU.add, ALU.mult).then_inc(s_lo.sem, 1)
                s_lo.wait(dve, b, i + 1)
                keep = part[:, 0:1] if i < NJ else part[:, 3:4]
                nc.vector.scalar_tensor_tensor(qk[:, i, :], hi[:, i % 2, :].bitcast(F32), keep, lo[:, i % 2, :], ALU.mult, ALU.add).then_inc(s_qk.sem, 1)

            def relative(b, n):
                s_r.wait(dve, b, n + 1)
                if n >= 2:
                    s_rw[n % 2].wait(dve, b, 32 * (n // 2))
                src = bank[:, 4 * (n % 2):4 * (n % 2) + 4, 0:2 * RW].rearrange("p g (t r) -> p g t r", t=2)[:, :, :, 0:NREL]
                nc.vector.tensor_copy(rl[:, n % 2, :, :, QL:QL + NREL], src).then_inc(s_rl[n % 2].sem, 1)

            def scores(b, n):
                qt, h = divmod(n, H)
                lo_c, hi_c = scores_window(qt)
                s_s.wait(dve, b, n + 1)
                hold(dve)
                if h == 0:
                    s_sk[qt % 2].wait(dve, b, 64 * (qt // 2 + 1))
                    hold(dve)
                if n >= 3:
                    s_t.wait(dve, b, n - 2)
                    hold(dve)
                nc.vector.tensor_tensor_reduce(sc[:, n % 3, OFF + lo_c:OFF + hi_c], bank[:, n % 4, lo_c:hi_c],
                                               skew[:, qt % 2, h, lo_c:hi_c], 1.0, -3e38, ALU.add, ALU.max,
                                               smax[:, n % 4:n % 4 + 1]).then_inc(s_sc.sem, 1)

            def normalize(b, qt):
                o = bank[:, 7, 0:H * (HD + 1)].rearrange("p (h d) -> p h d", h=H)
                s_pv.wait(dve, b, (qt + 1) * H)
                nc.vector.reciprocal(orec[:], o[:, :, HD]).then_inc(s_orec.sem, 1)
                s_orec.wait(dve, b, qt + 1)
                nc.vector.tensor_tensor(on[:, qt % 2], o[:, :, 0:HD], orec[:].unsqueeze(2).broadcast_to([P, H, HD]),
                                        ALU.mult).then_inc(s_on.sem, 1)

            def project(b, qt):
                s_y2.wait(dve, b, qt + 1)
                hold(dve)
                nc.vector.tensor_tensor(xt(b, qt), bank[:, slot("proj", qt), 0:D],
                                        xb[:, qt, :], ALU.add).then_inc(s_x2.sem, 1)

            with dve.Fori(0, B) as turn:
                b = (0, turn)
                ffn(b)
                layernorm(b, 1)
                s_v.wait(dve, b, 1)
                nc.vector.tensor_tensor(v[:, :, :, 0:HD],
                                        bank[:, 7, :].rearrange("p (t h d) -> p t h d", t=NT, h=H),
                                        bv[:].rearrange("p (h d) -> p h d", h=H).unsqueeze(1).broadcast_to([P, NT, H, HD]),
                                        ALU.add).then_inc(s_vb.sem, 1)
                for i in range(2 * NJ):
                    split(b, i)
                for n in range(0, NR, 2):
                    relative(b, n)
                s_qkvw.wait(dve, b, 32)
                hold(dve)
                s_rw[0].wait(dve, b, 32 * NR // 2)
                hold(dve)
            with dve.Fori(0, B) as turn:
                b = (1, turn)
                for t in range(NT):
                    nc.vector.tensor_tensor(xb[:, t, :], xt(b, t), bp[:], ALU.add).then_inc(s_xb.sem, 1)
                s_xb.wait(dve, b, NT)
                hold(dve)
                for kind, n in STEPS:
                    if kind == "score":
                        scores(b, n)
                    if kind == "norm":
                        normalize(b, n)
                    if kind == "add":
                        project(b, n)
                ffn(b)

        @block.scalar
        def _(act):
            act.wait_ge(s_w, 16 * 13)
            act.wait_ge(s_rel, 2)
            def flip(b, l):
                s_tr.wait(act, b, l + 1)
                nc.scalar.copy(xnT[:], bank[:, 6, :]).then_inc(s_xnT.sem, 1)

            def ffn(b):
                flip(b, 0)
                s_gl.wait(act, b, 2)
                nc.scalar.activation(gp[:], gl[:], ACT.Exp).then_inc(s_gp.sem, 1)
                for u, (xi, c) in enumerate(UNITS):
                    m = XC[xi][c][1]
                    n = u
                    s_h.wait(act, b, n + 1)
                    if u >= 2:
                        s_hs.wait(act, b, n - 1)
                    nc.scalar.activation(th[0:m, u % 2, :], bank[0:m, u % 2, :], ACT.Tanh, scale=0.5).then_inc(s_th.sem, 1)

            with act.Fori(0, B) as turn:
                b = (0, turn)
                ffn(b)
                flip(b, 1)
                for i in range(2 * NJ):
                    s_p.wait(act, b, i + 1)
                    if i >= 2:
                        s_qk.wait(act, b, i - 1)
                    if i < NJ:
                        nc.scalar.activation(hi[:, i % 2, :], bank[:, 4 + i % 2, :], ACT.Identity,
                                             bias=bq[:, i % NJ:i % NJ + 1]).then_inc(s_hi.sem, 1)
                    else:
                        nc.scalar.activation(hi[:, i % 2, :], bank[:, 4 + i % 2, :], ACT.Identity, scale=SCALE,
                                             bias=bks[:, i % NJ:i % NJ + 1]).then_inc(s_hi.sem, 1)
                for n in range(1, NR, 2):
                    s_r.wait(act, b, n + 1)
                    if n >= 2:
                        s_rw[n % 2].wait(act, b, 32 * (n // 2))
                    src = bank[:, 4 * (n % 2):4 * (n % 2) + 4, 0:2 * RW].rearrange("p g (t r) -> p g t r", t=2)[:, :, :, 0:NREL]
                    nc.scalar.copy(rl[:, n % 2, :, :, QL:QL + NREL], src).then_inc(s_rl[n % 2].sem, 1)
                s_rw[1].wait(act, b, 32 * NR // 2)
                hold(act)
            with act.Fori(0, B) as turn:
                b = (1, turn)
                for kind, n in STEPS:
                    if kind == "exp":
                        qt = n // H
                        w = len(QT_CHUNKS[qt]) * P
                        s_t.wait(act, b, n + 1)
                        if n >= 2:
                            s_pv.wait(act, b, n - 1)
                        nc.scalar.activation(pT[:, n % 2, 0:w], bank[:, slot("turn", n), 0:w], ACT.Exp).then_inc(s_pT.sem, 1)
                    if kind == "oT":
                        s_ot.wait(act, b, n + 1)
                        if n >= 2:
                            s_y2.wait(act, b, n - 1)
                        nc.scalar.copy(onT[:, n % 2, :], bank[:, slot("oT", n), 0:P]).then_inc(s_onT.sem, 1)
                ffn(b)
                s_acc.wait(act, b, E + 1)
                hold(act)
                act.dma_start(out_d[bass.ds(turn, 1)].rearrange("a (t p) d -> p (a t) d", p=P),
                             x[:, bass.ds(turn * NT, NT), :]).then_inc(s_out, 16)

        @block.tensor
        def _(pe):
            pe.wait_ge(s_cst, 7)
            pe.wait_ge(s_rel, 4)
            pe.wait_ge(s_w, 16 * 13)
            pe.wait_ge(s_wffn, 16 * (4 + 2 + 3))
            mm = nc.tensor.matmul
            def flip(b, l):
                s_xn.wait(pe, b, l + 1)
                for t in range(NT):
                    ins = nc.tensor.transpose(bank[:, 6, t * P:(t + 1) * P], xn[:, t, :], ident[:])
                ins.then_inc(s_tr.sem, 1)
                s_xnT.wait(pe, b, l + 1)

            def up(b, u):
                xi, c = UNITS[u]
                r, m = XC[xi][c]
                if u >= 2:
                    s_g.wait(pe, b, u - 1)
                a, g3 = (w1[:, xi - 1, r:r + m], w3[:, xi - 1, r:r + m]) if xi else (sw1[:, r:r + m], sw3[:, r:r + m])
                mm(bank[0:m, u % 2, :], a, xnT[:], start=True, stop=True)
                mm(bank[0:m, 2 + u % 2, :], g3, xnT[:], start=True, stop=True).then_inc(s_h.sem, 1)

            def down(b, xi):
                n = xi
                last = sum(len(XC[i]) for i in range(xi + 1))
                s_g.wait(pe, b, last)
                if xi >= 2:
                    s_acc.wait(pe, b, n - 1)
                for t in range(NT):
                    for c, (r, m) in enumerate(XC[xi]):
                        w = w2[0:m, xi - 1, c, :] if xi else sw2[0:m, c, :]
                        ins = mm(bank[:, 4 + xi % 2, t * D:(t + 1) * D], gT[0:m, xi % 2, c, t * P:(t + 1) * P], w,
                                 start=(c == 0), stop=(c == len(XC[xi]) - 1))
                ins.then_inc(s_y.sem, 1)

            def ffn(b):
                flip(b, 0)
                for t in range(NT):
                    ins = mm(bank[:, 7, t * E:(t + 1) * E], xnT[:, t * P:(t + 1) * P], gate[:], start=True, stop=True)
                ins.then_inc(s_gate.sem, 1)
                u = 0
                for xi in range(E + 1):
                    for c in range(len(XC[xi])):
                        up(b, u)
                        u += 1
                    if xi:
                        down(b, xi - 1)
                down(b, E)

            with pe.Fori(0, B) as turn:
                b = (0, turn)
                ffn(b)
                flip(b, 1)
                for t in range(NT):
                    ins = mm(bank[:, 7, t * D:(t + 1) * D], xnT[:, t * P:(t + 1) * P], wv[:], start=True, stop=True)
                ins.then_inc(s_v.sem, 1)
                for i in range(2 * NJ):
                    if i >= 2:
                        s_lo.wait(pe, b, i - 1)
                    w = (wq if i < NJ else wk)[:, i % NJ, :]
                    mm(bank[:, 4 + i % 2, :], w, xnT[:], start=True, stop=True).then_inc(s_p.sem, 1)
                for n in range(NR):
                    pair, j = divmod(n, NJ)
                    if n == 0:
                        s_qk.wait(pe, b, 2 * NJ)
                    if n == 1:
                        s_vb.wait(pe, b, 1)
                    if n >= 2:
                        s_rl[n % 2].wait(pe, b, n // 2)
                    for i in range(2):
                        for g in range(4):
                            r = slice(32 * g, 32 * g + 32)
                            q4 = qk[r, j, 2 * pair + i:N:4]
                            ins = mm(bank[:, 4 * (n % 2) + g, i * RW:(i + 1) * RW], q4, relr[r, j, :], start=True, stop=True)
                    ins.then_inc(s_r.sem, 1)
                for i in range(2):
                    s_rl[i].wait(pe, b, NR // 2)
                    hold(pe)
            with pe.Fori(0, B) as turn:
                b = (1, turn)

                def free_slot(kind, n):
                    i = TURNED.index((kind, n))
                    if i >= 3:
                        was, m = TURNED[i - 3]
                        {"turn": s_pT, "oT": s_onT, "proj": s_x2}[was].wait(pe, b, m + 1)

                for kind, n in STEPS:
                    qt, h = divmod(n, H)
                    if kind == "dot":
                        j, g = divmod(h, 4)
                        r = slice(32 * g, 32 * g + 32)
                        lo_c, hi_c = scores_window(qt)
                        k0 = qt * P - (REACH + 1)
                        if n >= 4:
                            s_sc.wait(pe, b, n - 3)
                        if h == 0:
                            for t in QT_CHUNKS[qt]:
                                s_tile[t].wait(pe, b, 32)
                                hold(pe)
                        ins = mm(bank[:, n % 4, lo_c:hi_c], qk[r, j, qt * P:(qt + 1) * P], qk[r, NJ + j, k0 + lo_c:k0 + hi_c],
                                 start=True, stop=True)
                        ins.then_inc(s_s.sem, 1)
                    if kind == "turn":
                        tiles = QT_CHUNKS[qt]
                        first = tiles[0] - qt + 1
                        out = bank[:, slot("turn", n), 0:len(tiles) * P]
                        free_slot("turn", n)
                        s_shift.wait(pe, b, n + 1)
                        mm(out.rearrange("p (c q) -> p c q", q=P), ones_b[:],
                           shift[:, n % 2, :].unsqueeze(1).broadcast_to([P, len(tiles), P]), start=True, stop=False)
                        for i in range(len(tiles)):
                            ins = mm(out[:, i * P:(i + 1) * P], sc[:, n % 3, (first + i) * P:(first + i + 1) * P], ident[:],
                                     start=False, stop=(i == len(tiles) - 1), is_transpose=True)
                        ins.then_inc(s_t.sem, 1)
                    if kind == "pv":
                        if h == 0 and qt:
                            s_on.wait(pe, b, qt)
                        s_pT.wait(pe, b, n + 1)
                        tiles = QT_CHUNKS[qt]
                        for i, kt in enumerate(tiles):
                            ins = mm(bank[:, 7, h * (HD + 1):(h + 1) * (HD + 1)], pT[:, n % 2, i * P:(i + 1) * P], v[:, kt, h, :],
                                     start=(i == 0), stop=(i == len(tiles) - 1))
                        ins.then_inc(s_pv.sem, 1)
                    if kind == "oT":
                        s_on.wait(pe, b, n + 1)
                        free_slot("oT", n)
                        nc.tensor.transpose(bank[:, slot("oT", n), 0:P], on[:, n % 2].rearrange("p h d -> p (h d)"),
                                            ident[:]).then_inc(s_ot.sem, 1)
                    if kind == "proj":
                        s_onT.wait(pe, b, n + 1)
                        free_slot("proj", n)
                        mm(bank[:, slot("proj", n), 0:D], onT[:, n % 2, :], wp[:], start=True,
                           stop=True).then_inc(s_y2.sem, 1)
                s_x2.wait(pe, b, NT)
                ffn(b)


_OUTS = [((B, N, D), "float32")]


def kernel(**inputs):
    import numpy as _np
    import concourse.bacc as _bacc
    from concourse import mybir as _mybir
    from concourse.bass_utils import run_bass_kernel_spmd as _run

    a = {k.replace("L0_", ""): _np.asarray(v) for k, v in inputs.items()}

    def copies(w):
        w = w.reshape(NJ, 4, 1, HD, -1)
        return _np.broadcast_to(w, (NJ, 4, 4, HD, w.shape[-1])).reshape(NJ, P, -1)

    wqkv, bqkv = a["attn_qkv_w"].reshape(3, D, D), a["attn_qkv_b"].reshape(3, D)
    rel = _np.zeros((H, HD, RW), _np.float32)
    rel[:, :, :NREL] = a["attn_rel_emb"].transpose(0, 2, 1)
    part = _np.zeros((4, 4, HD, 6), _np.float32)
    for c in range(4):
        for at, low in ((0, c % 2), (3, c // 2)):
            part[:, c, :, at] = -1.0 if low else 1.0
            part[:, c, :, 2 if at == 0 else 4] = 1.0 if low else 0.0
        part[:, c, :, 5] = SCALE * (c // 2)
    arrays = {
        "x": a["attn_x"], "gate": a["ffn_gate_w"].T, "w1": a["ffn_w1"], "w2": a["ffn_w2"], "w3": a["ffn_w3"],
        "sw1": a["ffn_sw1"], "sw2": a["ffn_sw2"], "sw3": a["ffn_sw3"],
        "wq": copies(wqkv[0]).transpose(2, 0, 1), "wk": copies(wqkv[1]).transpose(2, 0, 1), "wv": wqkv[2].T,
        "bq": copies(bqkv[0])[:, :, 0].T, "bk": copies(bqkv[1])[:, :, 0].T, "bv": _np.tile(bqkv[2], (P, 1)),
        "wp": a["attn_proj_w"].T, "bp": _np.tile(a["attn_proj_b"], (P, 1)),
        "rel": copies(rel.reshape(H * HD, RW)).transpose(1, 0, 2),
        "ident": _np.eye(P, dtype=_np.float32), "part": part.reshape(P, 6),
        "tri": _np.broadcast_to(_np.tril(_np.ones((E, E), _np.float32), -1), (P, E, E)),
    }
    nc = _bacc.Bacc("TRN2", target_bir_lowering=False, num_devices=1)
    by_name = {k: _np.ascontiguousarray(arrays[n]) for n in ("x", "gate", "w1", "w2", "w3", "sw1", "sw2", "sw3") for k in [n]}
    by_name.update({k: _np.ascontiguousarray(arrays[k]) for k in ("wq", "wk", "wv", "bq", "bk", "bv", "wp", "bp", "rel", "ident", "part", "tri")})
    args = [nc.dram_tensor(f"in_{k}", v.shape, _mybir.dt.from_np(v.dtype), kind="ExternalInput").ap() for k, v in by_name.items()]
    for i, (shape, dtype) in enumerate(_OUTS):
        args.append(nc.dram_tensor(f"out_{i}", shape, _mybir.dt.from_np(_np.dtype(dtype)), kind="ExternalOutput").ap())
    scratch = nc.dram_tensor("scratch", (B * NT * QS,), _mybir.dt.float32, kind="Internal").ap()
    qk = nc.dram_tensor("qk_rows", (B, P, 2 * NJ * N), _mybir.dt.float32, kind="Internal").ap()
    v = nc.dram_tensor("v_rows", (B, P, NT * H * (HD + 1)), _mybir.dt.float32, kind="Internal").ap()
    macaron_kernel(nc, *args, scratch, qk, v)
    r = _run(nc, [{f"in_{k}": v for k, v in by_name.items()}], core_ids=[0])
    return r.results[0]["out_0"]
```

```python
from contextlib import ExitStack

import concourse.bass as bass
from concourse import mybir

ALU = mybir.AluOpType
ACT = mybir.ActivationFunctionType
AX = mybir.AxisListType.X
F32 = mybir.dt.float32
F32R = mybir.dt.float32r
BF16 = mybir.dt.bfloat16

P = 128
B, N, D = 4, 512, 128
NT = N // P
E, EH, SH = 8, 352, 192
EPS = 1e-5
H, HD = 16, 8
NJ = H // 4
REACH = 99
NREL = 2 * REACH + 1
RW = NREL + 1
WIN = P + 2 * (REACH + 1)
OFF = P - (REACH + 1)
NEG = -1e8
QW = 232
QL = 32
QP = QL + NREL + QL + 1
ROW = H * QP
QS = P * (ROW + 1)
SCALE = float(1.0 / (8.0 ** 0.5))


def chunks(width):
    return [(c, min(P, width - c)) for c in range(0, width, P)]


EC, SC = chunks(EH), chunks(SH)
XC = [SC] + [EC] * E
UNITS = [(x, c) for x in range(E + 1) for c in range(len(XC[x]))]
NU = len(UNITS)
QT_CHUNKS = [[t for t in (qt - 1, qt, qt + 1) if 0 <= t < NT] for qt in range(NT)]


def head_steps():
    steps = []
    for n in range(NT * H + H):
        if n < NT * H:
            steps += [("dot", n), ("score", n)]
        if 0 <= n - 2 < NT * H:
            steps += [("turn", n - 2), ("exp", n - 2)]
        m = n - 3
        if 0 <= m < NT * H:
            steps.append(("pv", m))
            if m % H == H - 1:
                steps.append(("keep", m // H))
        if m >= H:
            qt = m // H - 1
            steps += {0: [("back", qt)], 2: [("norm", qt)], 4: [("oT", qt)], 6: [("proj", qt), ("add", qt)]}.get(m % H, [])
    return steps


STEPS = head_steps()
TURNED = [s for s in STEPS if s[0] in ("turn", "back", "oT", "proj")]


def slot(kind, n):
    return 4 + TURNED.index((kind, n)) % 3


class Count:

    def __init__(self, sem, *pers):
        self.sem, self.pers = sem, pers

    def wait_before(self, eng, b):
        k, turn = b
        eng.wait_ge(self.sem, turn * self.pers[k] + B * sum(self.pers[:k]))

    def wait(self, eng, b, n):
        k, turn = b
        eng.wait_ge(self.sem, turn * self.pers[k] + (B * sum(self.pers[:k]) + n))


def macaron_kernel(nc, x_d, gate_d, w1_d, w2_d, w3_d, sw1_d, sw2_d, sw3_d, wq_d, wk_d, wv_d, bq_d, bk_d, bv_d,
                   wp_d, bp_d, rel_d, ident_d, part_d, tri_d, out_d, scratch, qk_d, v_d):
    with ExitStack() as ctx:
        def sb(name, shape, dt=F32):
            return ctx.enter_context(nc.sbuf_tensor(name, shape, dt))

        def count(name, *pers):
            return Count(ctx.enter_context(nc.semaphore(name)), *pers)

        def sem(name):
            return ctx.enter_context(nc.semaphore(name))

        bank = ctx.enter_context(nc.psum_tensor("bank", [P, 8, 512], F32))

        w1 = sb("w1", [P, E, EH]); w3 = sb("w3", [P, E, EH]); w2 = sb("w2", [P, E, len(EC), D])
        sw1 = sb("sw1", [P, SH]); sw3 = sb("sw3", [P, SH]); sw2 = sb("sw2", [P, len(SC), D])
        gate = sb("gate", [P, E])
        wq = sb("wq", [P, NJ, P]); wk = sb("wk", [P, NJ, P]); wv = sb("wv", [P, D]); wp = sb("wp", [P, D])
        bq = sb("bq", [P, NJ]); bk = sb("bk", [P, NJ]); bks = sb("bks", [P, NJ]); bv = sb("bv", [P, D]); bp = sb("bp", [P, D])
        part = sb("part", [P, 6])
        rel = sb("rel", [P, NJ, RW]); rel_hi = sb("rel_hi", [P, NJ, RW], F32R); relr = sb("relr", [P, NJ, RW], F32R)
        ident = sb("ident", [P, P]);
        tri = sb("tri", [P, E, E])
        mhalf = sb("mhalf", [P, NT])
        x = sb("x", [P, B * NT, D])
        stats = sb("stats", [P, NT, 6]); mv = sb("mv", [P, NT, 2]); ve = sb("ve", [P, NT]); rstd = sb("rstd", [P, NT])
        xn = sb("xn", [P, NT, D]); xnT = sb("xnT", [P, N])
        gmax = sb("gmax", [P, NT]); gl = sb("gl", [P, NT, E]); gp = sb("gp", [P, NT, E]); gsum = sb("gsum", [P, NT])
        ginv = sb("ginv", [P, NT]); above = sb("above", [P, NT, E, E]); level = sb("level", [P, NT, E, E])
        rank = sb("rank", [P, NT, E]); comb = sb("comb", [P, NT, E])
        th = sb("th", [P, 2, N]); hs = sb("hs", [P, 2, N]); gT = sb("gT", [P, 2, len(EC), N]); acc = sb("acc", [P, NT, D])
        hi = sb("hi", [P, 2, N], F32R); lo = sb("lo", [P, 2, N])
        qk = sb("qk", [P, 2 * NJ, N], F32R); v = sb("v", [P, NT, H, HD + 1])
        NR = 2 * NJ
        band = sb("band", [P, NR * 4 * 2 * QP])
        rl = band[:].rearrange("p (n g t r) -> p n g t r", n=NR, g=4, t=2)
        skew = band[:, 0:2 * H * WIN].rearrange("p (a h w) -> p a h w", a=2, h=H)
        sc = sb("sc", [P, 3, 3 * P]); smax = sb("smax", [P, 4])
        pT = sb("pT", [P, 2, 3 * P])
        oT = sb("oT", [P, N]); orec = sb("orec", [P, H]); on = sb("on", [P, 2, H, HD]); onT = sb("onT", [P, 2, P]); xb = sb("xb", [P, NT, D])

        s_g0 = sem("s_g0"); s_wsh = sem("s_wsh"); s_w = sem("s_w"); s_wffn = sem("s_wffn"); s_x = sem("s_x"); s_cst = sem("s_cst"); s_fill = sem("s_fill"); s_rel = sem("s_rel")
        paced = sem("paced")
        s_stats = count("s_stats", 2 * NT, NT); s_mv = count("s_mv", 2 * NT, NT); s_ve = count("s_ve", 2, 1)
        s_rstd = count("s_rstd", 2, 1); s_xn = count("s_xn", 2, 1); s_tr = count("s_tr", 2, 1); s_xnT = count("s_xnT", 2, 1)
        s_gate = count("s_gate", 1, 1); s_gl = count("s_gl", 2, 2); s_gp = count("s_gp", 1, 1); s_gv = count("s_gv", 8, 8)
        s_comb = count("s_comb", 1, 1)
        s_h = count("s_h", NU, NU); s_th = count("s_th", NU, NU); s_hs = count("s_hs", NU, NU); s_g = count("s_g", NU, NU)
        s_y = count("s_y", E + 1, E + 1); s_acc = count("s_acc", E + 1, E + 1)
        s_v = count("s_v", 1); s_vb = count("s_vb", 1)
        s_p = count("s_p", 2 * NJ); s_hi = count("s_hi", 2 * NJ); s_lo = count("s_lo", 2 * NJ); s_qk = count("s_qk", 2 * NJ)
        s_r = count("s_r", NR); s_rl = [count(f"s_rl{i}", NR // 2) for i in range(2)]
        s_rw = [count(f"s_rw{i}", 32 * NR // 2, 0) for i in range(2)]
        s_qkvw = count("s_qkvw", 32, 0); s_flushed = sem("s_flushed"); s_band = sem("s_band")
        s_tile = [count(f"s_tile{i}", 0, 32) for i in range(NT)]
        s_sk = [count(f"s_sk{i}", 0, 64 * NT // 2) for i in range(2)]
        NH = NT * H
        s_s = count("s_s", 0, NH); s_sc = count("s_sc", 0, NH); s_low = count("s_low", 0, NH); s_t = count("s_t", 0, NH)
        s_pT = count("s_pT", 0, NH); s_pv = count("s_pv", 0, NH); s_orec = count("s_orec", 0, NT); s_on = count("s_on", 0, NT)
        s_xb = count("s_xb", 0, NT); s_ot = count("s_ot", 0, NT); s_onT = count("s_onT", 0, NT); s_y2 = count("s_y2", 0, NT)
        s_x2 = count("s_x2", 0, NT); s_keep = count("s_keep", 0, NT); s_back = count("s_back", 0, NT); s_out = sem("s_out")

        block = ctx.enter_context(nc.Block())

        def hold(eng):
            eng.sem_inc(paced, 1)

        def xt(b, t):
            return x[:, bass.ds(b[1] * NT + t, 1), :].rearrange("p a d -> p (a d)")

        def scores_window(qt):
            return (REACH + 1 if qt == 0 else 0), (WIN - (REACH + 1) if qt == NT - 1 else WIN)


        @block.sync
        def _(sp):
            for k in range(B):
                sp.dma_start(x[:, k * NT:(k + 1) * NT, :], x_d[k].rearrange("(t p) d -> p t d", p=P)).then_inc(s_x, 16)
                if k == 0:
                    for dst, src in ((ident, ident_d), (gate, gate_d), (tri, tri_d)):
                        sp.dma_start(dst[:], src).then_inc(s_g0, 16)
                    sp.dma_start(sw1[:], sw1_d).then_inc(s_wsh, 16)
                    sp.dma_start(sw3[:], sw3_d).then_inc(s_wsh, 16)
                    for c, (r, m) in enumerate(SC):
                        sp.dma_start(sw2[0:m, c, :], sw2_d[r:r + m, :]).then_inc(s_wsh, 16)
            sp.dma_start(w1[:], w1_d.rearrange("e d h -> d e h")).then_inc(s_wffn, 16)
            sp.dma_start(w3[:], w3_d.rearrange("e d h -> d e h")).then_inc(s_wffn, 16)
            for c, (r, m) in enumerate(EC):
                sp.dma_start(w2[0:m, :, c, :], w2_d[:, r:r + m, :].rearrange("e p d -> p e d")).then_inc(s_wffn, 16)
            for dst, src in ((wq, wq_d), (wk, wk_d), (wv, wv_d), (wp, wp_d), (bq, bq_d), (bk, bk_d), (bv, bv_d), (bp, bp_d),
                             (part, part_d), (rel, rel_d)):
                sp.dma_start(dst[:], src).then_inc(s_w, 16)
            sp.sem_inc(s_flushed, 1)
            with sp.Fori(0, B) as turn:
                b = (0, turn)
                s_vb.wait(sp, b, 1)
                hold(sp)
                s_qk.wait(sp, b, 2 * NJ)
                hold(sp)
                sp.dma_start(qk_d[bass.ds(turn, 1)].rearrange("a p f -> (a p) f"),
                             qk[:].bitcast(F32).rearrange("p j n -> p (j n)")).then_inc(s_qkvw.sem, 16)
                sp.dma_start(v_d[bass.ds(turn, 1)].rearrange("a p f -> (a p) f"),
                             v[:].rearrange("p t h d -> p (t h d)")).then_inc(s_qkvw.sem, 16)
                for n in range(NR):
                    pair, j = divmod(n, NJ)
                    s_rl[n % 2].wait(sp, b, n // 2 + 1)
                    hold(sp)
                    for i in range(2):
                        dst = bass.AP(scratch.tensor, scratch.offset + turn * QS + ((2 * pair + i) * NT * QS + 4 * j * QP),
                                      [[ROW + 1, P], [QP, 4], [1, QP - 1]])
                        sp.dma_start(dst, rl[:, n, :, i, 0:QP - 1]).then_inc(s_rw[n % 2].sem, 16)
                for i in range(2):
                    s_rw[i].wait(sp, b, 32 * NR // 2)
                    hold(sp)
                s_qkvw.wait(sp, b, 32)
                hold(sp)
                sp.sem_inc(s_flushed, 1)
            sp.wait_ge(s_band, 1)
            with sp.Fori(0, B) as turn:
                b = (1, turn)

                def load_tile(turn, t):
                    sp.dma_start(qk[:, :, t * P:(t + 1) * P].bitcast(F32),
                                 qk_d[bass.ds(turn, 1)].rearrange("a p (j n) -> (a p) j n", n=N)[:, :, t * P:(t + 1) * P])\
                        .then_inc(s_tile[t].sem, 16)
                    sp.dma_start(v[:, t].rearrange("p h d -> p (h d)"),
                                 v_d[bass.ds(turn, 1)].rearrange("a p (t f) -> (a p) t f", t=NT)[:, t, :])\
                        .then_inc(s_tile[t].sem, 16)

                s_tr.wait_before(sp, b)
                hold(sp)
                for qt in range(NT):
                    if qt == 0:
                        for t in range(NT):
                            load_tile(turn, t)
                    if qt >= 2:
                        s_sc.wait(sp, b, (qt - 1) * H)
                        hold(sp)
                    for a in range(4):
                        src = bass.AP(scratch.tensor, scratch.offset + turn * (NT * QS) + (qt * QS + 32 * a * (ROW + 1) + QL - 1),
                                      [[ROW, 32], [QP, H], [1, QW]])
                        sp.dma_start(skew[32 * a:32 * a + 32, qt % 2, :, 32 * a:32 * a + QW], src).then_inc(s_sk[qt % 2].sem, 16)

            sp.wait_ge(s_out, 16 * B)

        @block.gpsimd
        def _(pool):
            nc.gpsimd.memset(mhalf[:], -0.5).then_inc(s_cst, 1)
            pool.wait_ge(s_cst, 1)

            def rsqrt(b, l):
                s_ve.wait(pool, b, l + 1)
                nc.gpsimd.tensor_tensor(rstd[:], ve[:], mhalf[:], ALU.pow).then_inc(s_rstd.sem, 1)

            with pool.Fori(0, B) as turn:
                b = (0, turn)
                rsqrt(b, 0)
                rsqrt(b, 1)
            pool.wait_ge(s_flushed, B + 1)
            nc.gpsimd.memset(band[:, 0:2 * H * WIN], NEG).then_inc(s_band, 1)
            with pool.Fori(0, B) as turn:
                b = (1, turn)
                rsqrt(b, 0)

        @block.vector
        def _(dve):
            def layernorm(b, l):
                if l == 1:
                    s_acc.wait(dve, b, E + 1)
                    hold(dve)
                if b[0] == 1:
                    s_x2.wait(dve, b, NT)
                    hold(dve)
                for t in range(NT):
                    nc.vector.bn_stats(stats[:, t, :], xt(b, t)).then_inc(s_stats.sem, 1)
                s_stats.wait(dve, b, l * NT + NT)
                hold(dve)
                for t in range(NT):
                    nc.vector.bn_aggr(mv[:, t, :], stats[:, t, :]).then_inc(s_mv.sem, 1)
                s_mv.wait(dve, b, l * NT + NT)
                nc.vector.tensor_scalar(ve[:], mv[:, :, 1], EPS, None, ALU.add).then_inc(s_ve.sem, 1)
                s_rstd.wait(dve, b, l + 1)
                hold(dve)
                for t in range(NT):
                    ins = nc.vector.tensor_scalar(xn[:, t, :], xt(b, t), mv[:, t, 0:1],
                                                  rstd[:, t:t + 1], ALU.subtract, ALU.mult)
                ins.then_inc(s_xn.sem, 1)

            def gating(b):
                def step(ins, n):
                    ins.then_inc(s_gv.sem, 1)
                    s_gv.wait(dve, b, n)

                logits = bank[:, 7, 0:NT * E].rearrange("p (t e) -> p t e", e=E)
                s_gate.wait(dve, b, 1)
                nc.vector.tensor_reduce(gmax[:], logits, AX, ALU.max).then_inc(s_gl.sem, 1)
                s_gl.wait(dve, b, 1)
                nc.vector.tensor_tensor(gl[:], logits, gmax[:].unsqueeze(2).broadcast_to([P, NT, E]),
                                        ALU.subtract).then_inc(s_gl.sem, 1)
                s_gp.wait(dve, b, 1)
                other = gp[:].unsqueeze(2).broadcast_to([P, NT, E, E])
                own = gp[:].unsqueeze(3).broadcast_to([P, NT, E, E])
                step(nc.vector.tensor_tensor(above[:], other, own, ALU.is_gt), 1)
                step(nc.vector.tensor_tensor(level[:], other, own, ALU.is_ge), 2)
                step(nc.vector.tensor_tensor(level[:], level[:], tri[:].unsqueeze(1).broadcast_to([P, NT, E, E]),
                                             ALU.mult), 3)
                step(nc.vector.tensor_tensor(above[:], above[:], level[:], ALU.max), 4)
                nc.vector.tensor_reduce(rank[:], above[:], AX, ALU.add).then_inc(s_gv.sem, 1)
                nc.vector.tensor_reduce(gsum[:], gp[:], AX, ALU.add).then_inc(s_gv.sem, 1)
                s_gv.wait(dve, b, 6)
                nc.vector.reciprocal(ginv[:], gsum[:]).then_inc(s_gv.sem, 1)
                nc.vector.scalar_tensor_tensor(comb[:], rank[:], 1.5, gp[:], ALU.is_lt, ALU.mult).then_inc(s_gv.sem, 1)
                s_gv.wait(dve, b, 8)
                nc.vector.scalar_tensor_tensor(comb[:], comb[:], 0.25, ginv[:].unsqueeze(2).broadcast_to([P, NT, E]),
                                               ALU.mult, ALU.mult).then_inc(s_comb.sem, 1)

            def hidden(b, u):
                xi, c = UNITS[u]
                m = XC[xi][c][1]
                n = u
                s_th.wait(dve, b, n + 1)
                nc.vector.scalar_tensor_tensor(hs[0:m, u % 2, :], th[0:m, u % 2, :], 1.0, bank[0:m, u % 2, :],
                                               ALU.add, ALU.mult).then_inc(s_hs.sem, 1)
                s_hs.wait(dve, b, n + 1)
                nc.vector.tensor_tensor(gT[0:m, xi % 2, c, :], hs[0:m, u % 2, :], bank[0:m, 2 + u % 2, :],
                                        ALU.mult).then_inc(s_g.sem, 1)

            def gather(b, xi):
                n = xi
                s_y.wait(dve, b, n + 1)
                hold(dve)
                if xi == 1:
                    s_comb.wait(dve, b, 1)
                    hold(dve)
                if xi:
                    s_acc.wait(dve, b, n)
                    hold(dve)
                for t in range(NT):
                    w = comb[:, t, xi - 1:xi] if xi else 0.25
                    before = acc[:, t, :] if xi else xt(b, t)
                    after = acc[:, t, :] if xi < E else xt(b, t)
                    ins = nc.vector.scalar_tensor_tensor(after, bank[:, 4 + xi % 2, t * D:(t + 1) * D], w, before,
                                                         ALU.mult, ALU.add)
                ins.then_inc(s_acc.sem, 1)

            def ffn(b):
                layernorm(b, 0)
                gating(b)
                u = 0
                for xi in range(E + 1):
                    for c in range(len(XC[xi])):
                        hidden(b, u)
                        u += 1
                    if xi:
                        gather(b, xi - 1)
                gather(b, E)

            def split(b, i):
                wide = bank[:, 4 + i % 2, :]
                bias = (bq if i < NJ else bk)[:, i % NJ:i % NJ + 1]
                s_hi.wait(dve, b, i + 1)
                whole = part[:, 2:3] if i < NJ else part[:, 5:6]
                nc.vector.tensor_scalar(lo[:, i % 2, :], wide, bias, whole, ALU.add, ALU.mult).then_inc(s_lo.sem, 1)
                s_lo.wait(dve, b, i + 1)
                keep = part[:, 0:1] if i < NJ else part[:, 3:4]
                nc.vector.scalar_tensor_tensor(qk[:, i, :], hi[:, i % 2, :].bitcast(F32), keep, lo[:, i % 2, :], ALU.mult, ALU.add).then_inc(s_qk.sem, 1)

            def relative(b, n):
                s_r.wait(dve, b, n + 1)
                src = bank[:, 4 * (n % 2):4 * (n % 2) + 4, 0:2 * RW].rearrange("p g (t r) -> p g t r", t=2)[:, :, :, 0:NREL]
                nc.vector.tensor_copy(rl[:, n, :, :, QL:QL + NREL], src).then_inc(s_rl[n % 2].sem, 1)

            def scores(b, n):
                qt, h = divmod(n, H)
                lo_c, hi_c = scores_window(qt)
                s_s.wait(dve, b, n + 1)
                hold(dve)
                if h == 0:
                    s_sk[qt % 2].wait(dve, b, 64 * (qt // 2 + 1))
                    hold(dve)
                if n >= 3:
                    s_t.wait(dve, b, n - 2)
                    hold(dve)
                nc.vector.tensor_tensor_reduce(sc[:, n % 3, OFF + lo_c:OFF + hi_c], bank[:, n % 4, lo_c:hi_c],
                                               skew[:, qt % 2, h, lo_c:hi_c], 1.0, -3e38, ALU.add, ALU.max,
                                               smax[:, n % 4:n % 4 + 1]).then_inc(s_sc.sem, 1)
                s_sc.wait(dve, b, n + 1)
                nc.vector.tensor_scalar(sc[:, n % 3, OFF + lo_c:OFF + hi_c], sc[:, n % 3, OFF + lo_c:OFF + hi_c],
                                        smax[:, n % 4:n % 4 + 1], None, ALU.subtract).then_inc(s_low.sem, 1)

            def normalize(b, qt):
                o = bank[:, slot("back", qt), :].rearrange("p (h d) -> p h d", h=H)
                s_back.wait(dve, b, qt + 1)
                nc.vector.reciprocal(orec[:], o[:, :, HD]).then_inc(s_orec.sem, 1)
                s_orec.wait(dve, b, qt + 1)
                nc.vector.tensor_tensor(on[:, qt % 2], o[:, :, 0:HD], orec[:].unsqueeze(2).broadcast_to([P, H, HD]),
                                        ALU.mult).then_inc(s_on.sem, 1)

            def project(b, qt):
                s_y2.wait(dve, b, qt + 1)
                hold(dve)
                nc.vector.tensor_tensor(xt(b, qt), bank[:, slot("proj", qt), 0:D],
                                        xb[:, qt, :], ALU.add).then_inc(s_x2.sem, 1)

            nc.vector.memset(v[:], 1.0).then_inc(s_fill, 1)
            nc.vector.memset(sc[:], NEG).then_inc(s_fill, 1)
            for n in range(NR):
                nc.vector.memset(rl[:, n, :, :, 0:QL], NEG).then_inc(s_fill, 1)
                nc.vector.memset(rl[:, n, :, :, QL + NREL:QP], NEG).then_inc(s_fill, 1)
            dve.wait_ge(s_fill, 2 + 2 * NR)
            dve.wait_ge(s_w, 16 * 10)
            nc.vector.tensor_copy(rel_hi[:], rel[:]).then_inc(s_rel, 1)
            nc.vector.tensor_scalar(bks[:], bk[:], SCALE, None, ALU.mult).then_inc(s_rel, 1)
            dve.wait_ge(s_rel, 1)
            fl = "p j r -> p (j r)"
            nc.vector.tensor_scalar(rel[:], rel[:], part[:, 4:5], None, ALU.mult).then_inc(s_rel, 1)
            dve.wait_ge(s_rel, 3)
            nc.vector.scalar_tensor_tensor(relr[:].rearrange(fl), rel_hi[:].bitcast(F32).rearrange(fl), part[:, 3:4],
                                           rel[:].rearrange(fl), ALU.mult, ALU.add).then_inc(s_rel, 1)
            dve.wait_ge(s_x, 16 * B)
            with dve.Fori(0, B) as turn:
                b = (0, turn)
                ffn(b)
                layernorm(b, 1)
                dve.wait_ge(s_flushed, turn + 1)
                hold(dve)
                s_v.wait(dve, b, 1)
                nc.vector.tensor_tensor(v[:, :, :, 0:HD],
                                        bank[:, 7, :].rearrange("p (t h d) -> p t h d", t=NT, h=H),
                                        bv[:].rearrange("p (h d) -> p h d", h=H).unsqueeze(1).broadcast_to([P, NT, H, HD]),
                                        ALU.add).then_inc(s_vb.sem, 1)
                for i in range(2 * NJ):
                    split(b, i)
                for n in range(0, NR, 2):
                    relative(b, n)
            with dve.Fori(0, B) as turn:
                b = (1, turn)
                for t in range(NT):
                    nc.vector.tensor_tensor(xb[:, t, :], xt(b, t), bp[:], ALU.add).then_inc(s_xb.sem, 1)
                s_xb.wait(dve, b, NT)
                hold(dve)
                for kind, n in STEPS:
                    if kind == "score":
                        scores(b, n)
                    if kind == "norm":
                        normalize(b, n)
                    if kind == "add":
                        project(b, n)
                ffn(b)

        @block.scalar
        def _(act):
            def flip(b, l):
                s_tr.wait(act, b, l + 1)
                nc.scalar.copy(xnT[:], bank[:, 6, :]).then_inc(s_xnT.sem, 1)

            def ffn(b):
                flip(b, 0)
                s_gl.wait(act, b, 2)
                nc.scalar.activation(gp[:], gl[:], ACT.Exp).then_inc(s_gp.sem, 1)
                for u, (xi, c) in enumerate(UNITS):
                    m = XC[xi][c][1]
                    n = u
                    s_h.wait(act, b, n + 1)
                    if u >= 2:
                        s_hs.wait(act, b, n - 1)
                    nc.scalar.activation(th[0:m, u % 2, :], bank[0:m, u % 2, :], ACT.Tanh, scale=0.5).then_inc(s_th.sem, 1)

            with act.Fori(0, B) as turn:
                b = (0, turn)
                ffn(b)
                flip(b, 1)
                act.wait_ge(s_w, 16 * 10)
                act.wait_ge(s_rel, 2)
                for i in range(2 * NJ):
                    s_p.wait(act, b, i + 1)
                    if i >= 2:
                        s_qk.wait(act, b, i - 1)
                    if i < NJ:
                        nc.scalar.activation(hi[:, i % 2, :], bank[:, 4 + i % 2, :], ACT.Identity,
                                             bias=bq[:, i % NJ:i % NJ + 1]).then_inc(s_hi.sem, 1)
                    else:
                        nc.scalar.activation(hi[:, i % 2, :], bank[:, 4 + i % 2, :], ACT.Identity, scale=SCALE,
                                             bias=bks[:, i % NJ:i % NJ + 1]).then_inc(s_hi.sem, 1)
                for n in range(1, NR, 2):
                    s_r.wait(act, b, n + 1)
                    src = bank[:, 4 * (n % 2):4 * (n % 2) + 4, 0:2 * RW].rearrange("p g (t r) -> p g t r", t=2)[:, :, :, 0:NREL]
                    nc.scalar.copy(rl[:, n, :, :, QL:QL + NREL], src).then_inc(s_rl[n % 2].sem, 1)
            with act.Fori(0, B) as turn:
                b = (1, turn)
                for kind, n in STEPS:
                    if kind == "exp":
                        qt = n // H
                        w = len(QT_CHUNKS[qt]) * P
                        s_t.wait(act, b, n + 1)
                        if n >= 2:
                            s_pv.wait(act, b, n - 1)
                        nc.scalar.activation(pT[:, n % 2, 0:w], bank[:, slot("turn", n), 0:w], ACT.Exp).then_inc(s_pT.sem, 1)
                    if kind == "keep":
                        s_pv.wait(act, b, (n + 1) * H)
                        if n >= 1:
                            s_back.wait(act, b, n)
                        nc.scalar.copy(oT[:], bank[:, 7, :]).then_inc(s_keep.sem, 1)
                    if kind == "oT":
                        s_ot.wait(act, b, n + 1)
                        if n >= 2:
                            s_y2.wait(act, b, n - 1)
                        nc.scalar.copy(onT[:, n % 2, :], bank[:, slot("oT", n), 0:P]).then_inc(s_onT.sem, 1)
                ffn(b)
                s_acc.wait(act, b, E + 1)
                hold(act)
                act.dma_start(out_d[bass.ds(turn, 1)].rearrange("a (t p) d -> p (a t) d", p=P),
                             x[:, bass.ds(turn * NT, NT), :]).then_inc(s_out, 16)

        @block.tensor
        def _(pe):
            pe.wait_ge(s_g0, 16 * 3)
            mm = nc.tensor.matmul

            def flip(b, l):
                s_xn.wait(pe, b, l + 1)
                for t in range(NT):
                    ins = nc.tensor.transpose(bank[:, 6, t * P:(t + 1) * P], xn[:, t, :], ident[:])
                ins.then_inc(s_tr.sem, 1)
                s_xnT.wait(pe, b, l + 1)

            def up(b, u):
                xi, c = UNITS[u]
                r, m = XC[xi][c]
                if u >= 2:
                    s_g.wait(pe, b, u - 1)
                a, g3 = (w1[:, xi - 1, r:r + m], w3[:, xi - 1, r:r + m]) if xi else (sw1[:, r:r + m], sw3[:, r:r + m])
                mm(bank[0:m, u % 2, :], a, xnT[:], start=True, stop=True)
                mm(bank[0:m, 2 + u % 2, :], g3, xnT[:], start=True, stop=True).then_inc(s_h.sem, 1)

            def down(b, xi):
                n = xi
                last = sum(len(XC[i]) for i in range(xi + 1))
                s_g.wait(pe, b, last)
                if xi >= 2:
                    s_acc.wait(pe, b, n - 1)
                for t in range(NT):
                    for c, (r, m) in enumerate(XC[xi]):
                        w = w2[0:m, xi - 1, c, :] if xi else sw2[0:m, c, :]
                        ins = mm(bank[:, 4 + xi % 2, t * D:(t + 1) * D], gT[0:m, xi % 2, c, t * P:(t + 1) * P], w,
                                 start=(c == 0), stop=(c == len(XC[xi]) - 1))
                ins.then_inc(s_y.sem, 1)

            def ffn(b):
                flip(b, 0)
                for t in range(NT):
                    ins = mm(bank[:, 7, t * E:(t + 1) * E], xnT[:, t * P:(t + 1) * P], gate[:], start=True, stop=True)
                ins.then_inc(s_gate.sem, 1)
                pe.wait_ge(s_wsh, 16 * 4)
                u = 0
                for xi in range(E + 1):
                    for c in range(len(XC[xi])):
                        if u == len(SC):
                            pe.wait_ge(s_wffn, 16 * 5)
                        up(b, u)
                        u += 1
                    if xi:
                        down(b, xi - 1)
                down(b, E)

            with pe.Fori(0, B) as turn:
                b = (0, turn)
                ffn(b)
                flip(b, 1)
                pe.wait_ge(s_w, 16 * 10)
                pe.wait_ge(s_rel, 4)
                for t in range(NT):
                    ins = mm(bank[:, 7, t * D:(t + 1) * D], xnT[:, t * P:(t + 1) * P], wv[:], start=True, stop=True)
                ins.then_inc(s_v.sem, 1)
                for i in range(2 * NJ):
                    if i >= 2:
                        s_lo.wait(pe, b, i - 1)
                    w = (wq if i < NJ else wk)[:, i % NJ, :]
                    mm(bank[:, 4 + i % 2, :], w, xnT[:], start=True, stop=True).then_inc(s_p.sem, 1)
                for n in range(NR):
                    pair, j = divmod(n, NJ)
                    if n == 0:
                        s_qk.wait(pe, b, 2 * NJ)
                    if n == 1:
                        s_vb.wait(pe, b, 1)
                    if n >= 2:
                        s_rl[n % 2].wait(pe, b, n // 2)
                    for i in range(2):
                        for g in range(4):
                            r = slice(32 * g, 32 * g + 32)
                            q4 = qk[r, j, 2 * pair + i:N:4]
                            ins = mm(bank[:, 4 * (n % 2) + g, i * RW:(i + 1) * RW], q4, relr[r, j, :], start=True, stop=True)
                    ins.then_inc(s_r.sem, 1)
                for i in range(2):
                    s_rl[i].wait(pe, b, NR // 2)
                    hold(pe)
            with pe.Fori(0, B) as turn:
                b = (1, turn)

                def free_slot(kind, n):
                    i = TURNED.index((kind, n))
                    if i >= 3:
                        was, m = TURNED[i - 3]
                        {"turn": s_pT, "back": s_on, "oT": s_onT, "proj": s_x2}[was].wait(pe, b, m + 1)

                for kind, n in STEPS:
                    qt, h = divmod(n, H)
                    if kind == "dot":
                        j, g = divmod(h, 4)
                        r = slice(32 * g, 32 * g + 32)
                        lo_c, hi_c = scores_window(qt)
                        k0 = qt * P - (REACH + 1)
                        if n >= 4:
                            s_sc.wait(pe, b, n - 3)
                        if h == 0:
                            for t in QT_CHUNKS[qt]:
                                s_tile[t].wait(pe, b, 32)
                                hold(pe)
                        ins = mm(bank[:, n % 4, lo_c:hi_c], qk[r, j, qt * P:(qt + 1) * P], qk[r, NJ + j, k0 + lo_c:k0 + hi_c],
                                 start=True, stop=True)
                        ins.then_inc(s_s.sem, 1)
                    if kind == "turn":
                        tiles = QT_CHUNKS[qt]
                        first = tiles[0] - qt + 1
                        out = bank[:, slot("turn", n), 0:len(tiles) * P]
                        free_slot("turn", n)
                        s_low.wait(pe, b, n + 1)
                        for i in range(len(tiles)):
                            ins = nc.tensor.transpose(out[:, i * P:(i + 1) * P], sc[:, n % 3, (first + i) * P:(first + i + 1) * P],
                                                      ident[:])
                        ins.then_inc(s_t.sem, 1)
                    if kind == "pv":
                        if h == 0 and qt:
                            s_keep.wait(pe, b, qt)
                        s_pT.wait(pe, b, n + 1)
                        tiles = QT_CHUNKS[qt]
                        j, g = divmod(h, 4)
                        for i, kt in enumerate(tiles):
                            ins = mm(bank[32 * g:32 * g + HD + 1, 7, j * P:(j + 1) * P], v[:, kt, h, :],
                                     pT[:, n % 2, i * P:(i + 1) * P], start=(i == 0), stop=(i == len(tiles) - 1))
                        ins.then_inc(s_pv.sem, 1)
                    if kind == "back":
                        s_keep.wait(pe, b, n + 1)
                        free_slot("back", n)
                        for j in range(NJ):
                            ins = nc.tensor.transpose(bank[:, slot("back", n), j * P:(j + 1) * P], oT[:, j * P:(j + 1) * P], ident[:])
                        ins.then_inc(s_back.sem, 1)
                    if kind == "oT":
                        s_on.wait(pe, b, n + 1)
                        free_slot("oT", n)
                        nc.tensor.transpose(bank[:, slot("oT", n), 0:P], on[:, n % 2].rearrange("p h d -> p (h d)"),
                                            ident[:]).then_inc(s_ot.sem, 1)
                    if kind == "proj":
                        s_onT.wait(pe, b, n + 1)
                        free_slot("proj", n)
                        mm(bank[:, slot("proj", n), 0:D], onT[:, n % 2, :], wp[:], start=True,
                           stop=True).then_inc(s_y2.sem, 1)
                s_x2.wait(pe, b, NT)
                ffn(b)


_OUTS = [((B, N, D), "float32")]


def kernel(**inputs):
    import numpy as _np
    import concourse.bacc as _bacc
    from concourse import mybir as _mybir
    from concourse.bass_utils import run_bass_kernel_spmd as _run

    a = {k.replace("L0_", ""): _np.asarray(v) for k, v in inputs.items()}

    def copies(w):
        w = w.reshape(NJ, 4, 1, HD, -1)
        return _np.broadcast_to(w, (NJ, 4, 4, HD, w.shape[-1])).reshape(NJ, P, -1)

    wqkv, bqkv = a["attn_qkv_w"].reshape(3, D, D), a["attn_qkv_b"].reshape(3, D)
    rel = _np.zeros((H, HD, RW), _np.float32)
    rel[:, :, :NREL] = a["attn_rel_emb"].transpose(0, 2, 1)
    part = _np.zeros((4, 4, HD, 6), _np.float32)
    for c in range(4):
        for at, low in ((0, c % 2), (3, c // 2)):
            part[:, c, :, at] = -1.0 if low else 1.0
            part[:, c, :, 2 if at == 0 else 4] = 1.0 if low else 0.0
        part[:, c, :, 5] = SCALE * (c // 2)
    arrays = {
        "x": a["attn_x"], "gate": a["ffn_gate_w"].T, "w1": a["ffn_w1"], "w2": a["ffn_w2"], "w3": a["ffn_w3"],
        "sw1": a["ffn_sw1"], "sw2": a["ffn_sw2"], "sw3": a["ffn_sw3"],
        "wq": copies(wqkv[0]).transpose(2, 0, 1), "wk": copies(wqkv[1]).transpose(2, 0, 1), "wv": wqkv[2].T,
        "bq": copies(bqkv[0])[:, :, 0].T, "bk": copies(bqkv[1])[:, :, 0].T, "bv": _np.tile(bqkv[2], (P, 1)),
        "wp": a["attn_proj_w"].T, "bp": _np.tile(a["attn_proj_b"], (P, 1)),
        "rel": copies(rel.reshape(H * HD, RW)).transpose(1, 0, 2),
        "ident": _np.eye(P, dtype=_np.float32), "part": part.reshape(P, 6),
        "tri": _np.broadcast_to(_np.tril(_np.ones((E, E), _np.float32), -1), (P, E, E)),
    }
    nc = _bacc.Bacc("TRN2", target_bir_lowering=False, num_devices=1)
    by_name = {k: _np.ascontiguousarray(arrays[n]) for n in ("x", "gate", "w1", "w2", "w3", "sw1", "sw2", "sw3") for k in [n]}
    by_name.update({k: _np.ascontiguousarray(arrays[k]) for k in ("wq", "wk", "wv", "bq", "bk", "bv", "wp", "bp", "rel", "ident", "part", "tri")})
    args = [nc.dram_tensor(f"in_{k}", v.shape, _mybir.dt.from_np(v.dtype), kind="ExternalInput").ap() for k, v in by_name.items()]
    for i, (shape, dtype) in enumerate(_OUTS):
        args.append(nc.dram_tensor(f"out_{i}", shape, _mybir.dt.from_np(_np.dtype(dtype)), kind="ExternalOutput").ap())
    scratch = nc.dram_tensor("scratch", (B * NT * QS,), _mybir.dt.float32, kind="Internal").ap()
    qk = nc.dram_tensor("qk_rows", (B, P, 2 * NJ * N), _mybir.dt.float32, kind="Internal").ap()
    v = nc.dram_tensor("v_rows", (B, P, NT * H * (HD + 1)), _mybir.dt.float32, kind="Internal").ap()
    macaron_kernel(nc, *args, scratch, qk, v)
    r = _run(nc, [{f"in_{k}": v for k, v in by_name.items()}], core_ids=[0])
    return r.results[0]["out_0"]
```

```python
from contextlib import ExitStack

import concourse.bass as bass
from concourse import mybir

ALU = mybir.AluOpType
ACT = mybir.ActivationFunctionType
AX = mybir.AxisListType.X
F32 = mybir.dt.float32
F32R = mybir.dt.float32r

P = 128
B, N, D = 4, 512, 128
NT = N // P
E, EH, SH = 8, 352, 192
EPS = 1e-5
H, HD = 16, 8
NJ = H // 4
REACH = 99
NREL = 2 * REACH + 1
RW = NREL + 1
WIN = P + 2 * (REACH + 1)
OFF = P - (REACH + 1)
NEG = -1e8
QW = 232
QL = 32
QP = QL + NREL + QL + 1
ROW = H * QP
QS = P * (ROW + 1)
SCALE = float(1.0 / (8.0 ** 0.5))


def chunks(width):
    return [(c, min(P, width - c)) for c in range(0, width, P)]


EC, SC = chunks(EH), chunks(SH)
XC = [SC] + [EC] * E
UNITS = [(x, c) for x in range(E + 1) for c in range(len(XC[x]))]
NU = len(UNITS)
WUP = SH + E * EH
WUP_AT = [0] + [SH + e * EH for e in range(E)]
WUP_PARTS = [(0, SH)] + [(SH + i * 2 * EH, SH + (i + 1) * 2 * EH) for i in range(E // 2)]
SMALL_AT = [0, E, E + 6, E + 6 + NJ, E + 6 + 2 * NJ, E + 6 + 2 * NJ + E * E]
WIDE_AT = [0, NJ * P, 2 * NJ * P] + [2 * NJ * P + i * D for i in range(1, 5)]
H_BANKS = [(0, 2), (1, 3), (6, 7)]
GATE_STAGES = 7
NSLOT = 5
QT_CHUNKS = [[t for t in (qt - 1, qt, qt + 1) if 0 <= t < NT] for qt in range(NT)]


FIRST, MERGED, LAST, HEADS, BOTH, TAIL = range(6)
TURNS = (1, B - 1, 1, 1, B - 1, 1)

PIECES = 8 * NJ
NR = 2 * NJ
SIDE = [("gate", 0), ("flip", 0), ("v", 0)] + [("proj", i) for i in range(NJ)]
for i in range(NJ):
    SIDE += [("piece", 4 * i + g) for g in range(4)] + [("proj", NJ + i)]
SIDE += [("piece", m) for m in range(4 * NJ, PIECES)]

QK_OUT = 5


def merged_order():
    order, k = [], 1
    for u, (xi, c) in enumerate(UNITS):
        order.append(("unit", u))
        if u == 0:
            order.append(("side", 0))
        if u >= 2:
            order.append(("side", k))
            k += 1
        order.append(("hidden", u))
        order += [("split", SIDE[i][1]) for i in (k - 2, k - 1) if u >= 2 and i >= 0 and SIDE[i][0] == "proj"]
        if xi and c:
            order += [("down", (xi - 1, c - 1)), ("side", k)]
            k += 1
    order += [("side", i) for i in range(k, len(SIDE))]
    order += [("down", (E, 0)), ("down", (E, 1))]
    done = [step for n, step in enumerate(order) if step[0] != "split" or step not in order[:n]]
    assert sum(kind == "split" for kind, _ in done) == 2 * NJ
    return done


ORDER = merged_order()
AHEAD = (15, 18)
FILL_AT = (5, 7, 9, 11)


def on_scalar(m):
    return m % 4 != 0


def moved(m):
    act = sum(on_scalar(k) for k in range(m + 1))
    return (m + 1 - act, act)


def rl_slot(n):
    return (n - (NR - NSLOT)) % NSLOT


LAST_SLOT = (0, 1, 2, 3, 0, 1, 4, 3)
BAND_FREE = 7


def last_uses(n):
    return LAST_SLOT[:n].count(LAST_SLOT[n])


def side_bank(section, k):
    return 7 - k % 2 if section == MERGED else k % 8


def h_banks(section, u):
    if section == BOTH:
        return (2 * u % 3, (2 * u + 1) % 3)
    return H_BANKS[u % 2] if section == MERGED else H_BANKS[u % 3]


def head_steps(norm_at):
    turns = []
    for n in range(NT * H + 13):
        steps = []
        if n < NT * H:
            steps += [("dot", n), ("score", n)]
        if 0 <= n - 1 < NT * H:
            steps.append(("low", n - 1))
        if 0 <= n - 3 < NT * H:
            steps += [("turn", n - 3), ("exp", n - 3)]
        m = n - 5
        if 0 <= m < NT * H:
            steps.append(("pv", m))
            if m % H == H - 1:
                steps.append(("keep", m // H))
        if m >= H:
            qt = m // H - 1
            if m % H == 0:
                steps.append(("back", qt))
            if m % H == norm_at:
                steps.append(("norm", qt))
            steps += {4: [("oT", qt)], 6: [("proj", qt), ("add", qt)], 7: [("stat", qt)]}.get(m % H, [])
        turns.append([s for s in steps if 0 <= s[1]])
    return turns


STEPS = {HEADS: head_steps(2), BOTH: head_steps(0)}
TURNED = [s for turn in STEPS[HEADS] for s in turn if s[0] in ("turn", "back", "oT", "proj")]


SPARE = 3


def both_order():
    turn = iter(range(len(STEPS[BOTH])))
    order, beside = [], []
    slots = 2 + 2 * NU + NT * (E + 1) - SPARE

    def heads(times=1):
        for _ in range(times):
            i = sum(kind == "heads" for kind, _ in order)
            used = (i + 1) * len(STEPS[BOTH]) // slots > i * len(STEPS[BOTH]) // slots and i < slots
            n = next(turn) if used else None
            order.append(("heads", n))
            order.extend(beside)
            beside.clear()
            order.append(("after", n))
            if n == len(STEPS[BOTH]) - 1:
                order.append(("variances", 0))
                beside.append(("standardize", 0))

    order.append(("flip", 0))
    beside.append(("low_part", 0))
    heads(2)
    for u, (xi, c) in enumerate(UNITS):
        for half in range(2):
            order.append(("up", (u, half)))
            if half:
                beside.append(("hidden", u))
            elif 1 <= u <= GATE_STAGES:
                beside.append(("gating", u - 1))
            heads()
        if xi and c:
            for t in (2 * c - 2, 2 * c - 1):
                order.append(("down", (xi - 1, t)))
                if t == NT - 1:
                    beside.append(("gather", xi - 1))
                heads()
    for t in range(NT):
        order.append(("down", (E, t)))
        if t == NT - 1:
            beside.append(("gather", E))
        heads()
    assert next(turn, None) is None
    return order


BOTH_ORDER = both_order()


def slot(section, kind, n):
    return 6 if section == BOTH else 4 + TURNED.index((kind, n)) % 3


def dot_bank(section, n):
    return 4 + n % 2 if section == BOTH else n % 4


def y_bank(section, xi):
    return 3 if section == BOTH else 4 + xi % 2


def gate_bank(section):
    return 3 if section == BOTH else 7


def flip_bank(section):
    return 2 if section == BOTH else 6


class Count:

    def __init__(self, sem, *pers):
        self.sem, self.pers = sem, pers

    def start(self, b):
        k, turn = b
        return turn * self.pers[k] if k in (MERGED, BOTH) else 0, sum(t * p for t, p in zip(TURNS[:k], self.pers[:k]))

    def before(self, b):
        at, base = self.start(b)
        return at + base

    def at(self, b, n):
        at, base = self.start(b)
        return at + (base + n)


def macaron_kernel(nc, x_d, w1_d, w2_d, w3_d, sw1_d, sw2_d, sw3_d, small_d, wide_d, rel_d, ident_d, out_d,
                   scratch, qk_d, v_d):
    with ExitStack() as ctx:
        def sb(name, shape, dt=F32):
            return ctx.enter_context(nc.sbuf_tensor(name, shape, dt))

        def count(name, *pers):
            return Count(ctx.enter_context(nc.semaphore(name)), *pers)

        def sem(name):
            return ctx.enter_context(nc.semaphore(name))

        bank = ctx.enter_context(nc.psum_tensor("bank", [P, 8, 512], F32))

        w1_hi = sb("w1_hi", [P, WUP], F32R); w1_lo = sb("w1_lo", [P, WUP], F32R)
        w3_hi = sb("w3_hi", [P, WUP], F32R); w3_lo = sb("w3_lo", [P, WUP], F32R)
        w2 = sb("w2", [P, E, len(EC), D]); sw2 = sb("sw2", [P, len(SC), D])
        small = sb("small", [P, E + 6 + 2 * NJ + E * E])
        gate, part, bq, bk, tri = (small[:, c0:c1] for c0, c1 in zip(SMALL_AT, SMALL_AT[1:]))
        tri = tri.rearrange("p (a b) -> p a b", a=E)
        wide = sb("wide", [P, WIDE_AT[-1]])
        wq, wk, wv, wp, bv, bp = (wide[:, c0:c1] for c0, c1 in zip(WIDE_AT, WIDE_AT[1:]))
        wq = wq.rearrange("p (j c) -> p j c", j=NJ); wk = wk.rearrange("p (j c) -> p j c", j=NJ)
        bks = sb("bks", [P, NJ]); bq_lo = sb("bq_lo", [P, NJ]); bk_lo = sb("bk_lo", [P, NJ])
        rel = sb("rel", [P, NJ, RW]); rel_hi = sb("rel_hi", [P, NJ, RW], F32R); relr = sb("relr", [P, NJ, RW], F32R)
        ident = sb("ident", [P, P])
        mhalf = sb("mhalf", [P, NT])
        x = sb("x", [P, (B + 1) * NT, D])
        stats = sb("stats", [P, NT, 6]); mv = sb("mv", [P, NT, 2]); ve = sb("ve", [P, NT]); rstd = sb("rstd", [P, NT])
        xn = sb("xn", [P, 2, NT, D]); xnT = sb("xnT", [P, N]); xnT2 = sb("xnT2", [P, N]); xhi = sb("xhi", [P, N], F32R); xlo = sb("xlo", [P, N], F32R)
        gmax = sb("gmax", [P, NT]); gl = sb("gl", [P, NT, E]); gp = sb("gp", [P, NT, E]); gsum = sb("gsum", [P, NT])
        ginv = sb("ginv", [P, NT]); above = sb("above", [P, NT, E, E]); level = sb("level", [P, NT, E, E])
        rank = sb("rank", [P, NT, E]); comb = sb("comb", [P, NT, E])
        group = 4 * 2 * QP
        th_and_hs = sb("th_and_hs", [P, max(4 * N, group)])
        th = th_and_hs[:, 0:2 * N].rearrange("p (a n) -> p a n", a=2)
        hs = th_and_hs[:, 2 * N:4 * N].rearrange("p (a n) -> p a n", a=2)
        gT = sb("gT", [P, 2, len(EC), N]); acc = sb("acc", [P, NT, D])
        hi = sb("hi", [P, 2, N], F32R); lo = sb("lo", [P, 2, N])
        qk = sb("qk", [P, 2 * NJ, N], F32R); v = sb("v", [P, NT, H, HD + 1])
        band = sb("band", [P, max(NSLOT * 4 * 2 * QP, 2 * H * WIN)])
        rl = band[:, 0:NSLOT * 4 * 2 * QP].rearrange("p (n g t r) -> p n g t r", n=NSLOT, g=4, t=2)
        w1 = band[:, 0:WUP]; w3 = band[:, WUP:2 * WUP]
        skew = band[:, 0:2 * H * WIN].rearrange("p (a h w) -> p a h w", a=2, h=H)
        scores_and_probs = sb("scores_and_probs", [P, 7 * 3 * P]); smax = sb("smax", [P, 4])
        sc = scores_and_probs[:, 0:4 * 3 * P].rearrange("p (n k) -> p n k", n=4)
        pT = scores_and_probs[:, 4 * 3 * P:].rearrange("p (n k) -> p n k", n=3)
        last_rl = [held.rearrange("p (g t r) -> p g t r", g=4, t=2) for held in (
            band[:, (NSLOT - 2) * group:(NSLOT - 1) * group], band[:, (NSLOT - 1) * group:NSLOT * group],
            scores_and_probs[:, 0:group], gT[:].rearrange("p a c n -> p (a c n)")[:, 0:group], th_and_hs[:, 0:group])]
        oT = sb("oT", [P, N]); orec = sb("orec", [P, H]); on = sb("on", [P, 2, H, HD]); onT = sb("onT", [P, 2, P]); xb = sb("xb", [P, NT, D])

        s_g0 = sem("s_g0"); s_x0 = sem("s_x0"); s_x = sem("s_x"); s_rp = sem("s_rp"); s_w = sem("s_w")
        s_wsh = sem("s_wsh"); s_wup = sem("s_wup"); s_wdown = sem("s_wdown"); s_whi = sem("s_whi"); s_wlo = sem("s_wlo")
        s_edge = sem("s_edge"); s_cst = sem("s_cst"); s_fill = sem("s_fill"); s_rel = sem("s_rel")
        paced = sem("paced")
        def in_ffn(name, n):
            return count(name, n, n, 0, 0, n, n)

        def in_side(name, n):
            return count(name, 0, n, n, 0, 0, 0)

        def in_heads(name, n):
            return count(name, 0, 0, 0, n, n, 0)

        s_stats = count("s_stats", 2 * NT, 2 * NT, NT, NT, NT, 0); s_mv = count("s_mv", 2 * NT, 2 * NT, NT, NT, NT, 0)
        s_ve = count("s_ve", 2, 2, 1, 1, 1, 0); s_rstd = count("s_rstd", 2, 2, 1, 1, 1, 0)
        s_xn = count("s_xn", 2 * NT, 2 * NT, NT, NT, NT, 0)
        s_tr, s_xnT, s_xhi, s_xlo = (in_ffn(name, 1) for name in ("s_tr", "s_xnT", "s_xhi", "s_xlo"))
        s_tr2 = in_side("s_tr2", 1); s_xnT2 = in_side("s_xnT2", 1)
        s_gate = in_ffn("s_gate", 1); s_gl = in_ffn("s_gl", 2); s_gp = in_ffn("s_gp", 1); s_gv = in_ffn("s_gv", 8)
        s_comb = in_ffn("s_comb", 1)
        s_h, s_th, s_hs, s_g = (in_ffn(name, NU) for name in ("s_h", "s_th", "s_hs", "s_g"))
        s_y = in_ffn("s_y", E + 1); s_acc = in_ffn("s_acc", E + 1)
        s_v = in_side("s_v", 1); s_vb = in_side("s_vb", 1)
        s_p, s_hi, s_lo, s_qk = (in_side(name, 2 * NJ) for name in ("s_p", "s_hi", "s_lo", "s_qk"))
        s_r = in_side("s_r", PIECES)
        s_rl = [count(f"s_rl{i}", 0, moved(PIECES - 1)[i], moved(PIECES - 1)[i], 0, 0, 0) for i in range(2)]
        s_rw = [count(f"s_rw{i}", 32, 32 * len(range(i, NR, NSLOT)), 0, 0, 0, 0) for i in range(NSLOT)]
        s_lw = [sem(f"s_lw{i}") for i in range(len(last_rl))]; s_pad = sem("s_pad")
        s_qkvw = count("s_qkvw", 32, 32, 0, 0, 0, 0); s_band = sem("s_band")
        s_tile = [in_heads(f"s_tile{i}", 32) for i in range(NT)]
        s_sk = [in_heads(f"s_sk{i}", 64 * NT // 2) for i in range(2)]
        s_s, s_sc, s_t, s_pT, s_pv = (in_heads(name, NT * H) for name in ("s_s", "s_sc", "s_t", "s_pT", "s_pv"))
        s_low = [in_heads(f"s_low{i}", NT * H // 2) for i in range(2)]
        s_orec, s_on, s_xb, s_ot, s_onT, s_y2, s_x2, s_keep, s_back = (
            in_heads(name, NT) for name in ("s_orec", "s_on", "s_xb", "s_ot", "s_onT", "s_y2", "s_x2", "s_keep", "s_back"))
        s_out = sem("s_out")

        block = ctx.enter_context(nc.Block())

        def hold(eng):
            eng.sem_inc(paced, 1)

        def ffn_row(b):
            return {FIRST: (0, 1, 0), MERGED: (b[1], 1, 1), BOTH: (b[1], -1, B - 1), TAIL: (0, 1, 0)}[b[0]]

        def head_row(b):
            return (b[1], -1, B - 2) if b[0] == BOTH else (0, 1, B - 1)

        def side_row(b):
            return (b[1], 1, 0) if b[0] == MERGED else (0, 1, B - 1)

        def row_ahead(b):
            return (b[1], 1, 2) if b[0] == MERGED else (0, 1, 1)

        def xt(row, t):
            turn, factor, first = row
            return x[:, bass.ds(turn * (factor * NT) + (first * NT + t), 1), :].rearrange("p a d -> p (a d)")

        def left_bank(eng, b, k):
            kind, i = SIDE[k]
            if kind == "piece":
                who = on_scalar(i)
                eng.wait_ge(s_rl[who].sem, s_rl[who].at(b, moved(i)[who]))
            elif kind == "proj":
                eng.wait_ge(s_lo.sem, s_lo.at(b, i + 1))
            else:
                read = {"gate": s_gl, "flip": s_xnT2, "v": s_vb}[kind]
                eng.wait_ge(read.sem, read.at(b, 2 if kind == "gate" else 1))

        def scores_window(qt):
            return (REACH + 1 if qt == 0 else 0), (WIN - (REACH + 1) if qt == NT - 1 else WIN)


        def held(b, n):
            return last_rl[LAST_SLOT[n]] if b[0] == LAST else rl[:, rl_slot(n)]

        def piece(b, k):
            n, g = divmod(SIDE[k][1], 4)
            return (held(b, n)[:, g, :, QL:QL + NREL],
                    bank[:, side_bank(b[0], k), 0:2 * RW].rearrange("p (t r) -> p t r", t=2)[:, :, 0:NREL])

        def slot_written(eng, b, k):
            n = SIDE[k][1] // 4
            if b[0] == LAST:
                if last_uses(n):
                    eng.wait_ge(s_lw[LAST_SLOT[n]], 32 * last_uses(n))
                elif LAST_SLOT[n] < 2:
                    before = s_rw[(NR - 2 + LAST_SLOT[n]) % NSLOT]
                    eng.wait_ge(before.sem, before.before(b))
                elif LAST_SLOT[n] > 2:
                    eng.wait_ge(s_y.sem, s_y.before(b))
            else:
                eng.wait_ge(s_rw[n % NSLOT].sem, s_rw[n % NSLOT].at(b, n // NSLOT * 32))
                hold(eng)

        def scores_of(n):
            lo_c, hi_c = scores_window(n // H)
            return sc[:, n % 4, OFF + lo_c:OFF + hi_c]

        def out_of_reach(i, a):
            rows = slice(32 * a, 32 * a + 32)
            return [skew[rows, i, :, c0:c1] for c0, c1 in ((0, 32 * a), (32 * a + QW, WIN)) if c0 < c1]

        def left_band(eng, i):
            for rw in s_rw:
                eng.wait_ge(rw.sem, rw.before((LAST, 0)))
            if i:
                for k in range(2):
                    eng.wait_ge(s_lw[k], 32 * LAST_SLOT.count(k))

        @block.sync
        def _(sp):
            def load_x(k, loaded):
                sp.dma_start(x[:, k * NT:(k + 1) * NT, :], x_d[k].rearrange("(t p) d -> p t d", p=P)).then_inc(loaded, 16)

            load_x(0, s_x0)
            sp.dma_start(ident[:], ident_d).then_inc(s_g0, 16)
            sp.dma_start(w1[:, 0:SH], sw1_d).then_inc(s_wsh, 16)
            sp.dma_start(w3[:, 0:SH], sw3_d).then_inc(s_wsh, 16)
            for dst, src in ((w1, w1_d), (w3, w3_d)):
                sp.dma_start(dst[:, SH:].rearrange("p (e h) -> p e h", e=E), src.rearrange("e d h -> d e h")).then_inc(s_wup, 16)
            for c, (r, m) in enumerate(SC):
                sp.dma_start(sw2[0:m, c, :], sw2_d[r:r + m, :]).then_inc(s_wdown, 16)
            for c, (r, m) in enumerate(EC):
                sp.dma_start(w2[0:m, :, c, :], w2_d[:, r:r + m, :].rearrange("e p d -> p e d")).then_inc(s_wdown, 16)
            sp.dma_start(wide[:], wide_d).then_inc(s_w, 16)
            for k in range(1, B):
                load_x(k, s_x)
            sp.sem_inc(s_qkvw.sem, 32)
            for i in range(NSLOT):
                sp.sem_inc(s_rw[i].sem, 32)
            sp.wait_ge(s_edge, 2 * NSLOT)

            def save(b, last):
                turn = b[1] if b[0] == MERGED else B - 1
                for n in range(NR):
                    j, pair = divmod(n, 2)
                    for i in range(2):
                        sp.wait_ge(s_rl[i].sem, s_rl[i].at(b, moved(4 * n + 3)[i]))
                        hold(sp)
                    if last and n == 2:
                        sp.wait_ge(s_pad, 6)
                    if last and n == BAND_FREE:
                        left_band(sp, 1)
                        load_skew(head_row((HEADS, 0)), 1)
                    for i in range(2):
                        dst = bass.AP(scratch.tensor, scratch.offset + turn * QS + ((2 * pair + i) * NT * QS + 4 * j * QP),
                                      [[ROW + 1, P], [QP, 4], [1, QP - 1]])
                        written = s_lw[LAST_SLOT[n]] if last else s_rw[n % NSLOT].sem
                        sp.dma_start(dst, held(b, n)[:, :, i, 0:QP - 1]).then_inc(written, 16)
                    if n == QK_OUT:
                        sp.wait_ge(s_qk.sem, s_qk.at(b, 2 * NJ))
                        hold(sp)
                        sp.wait_ge(s_vb.sem, s_vb.at(b, 1))
                        hold(sp)
                        if last:
                            for t in range(NT):
                                sp.sem_inc(s_tile[t].sem, 32)
                        else:
                            sp.dma_start(qk_d[bass.ds(turn, 1)].rearrange("a p f -> (a p) f"),
                                         qk[:].bitcast(F32).rearrange("p j n -> p (j n)")).then_inc(s_qkvw.sem, 16)
                            sp.dma_start(v_d[bass.ds(turn, 1)].rearrange("a p f -> (a p) f"),
                                         v[:].rearrange("p t h d -> p (t h d)")).then_inc(s_qkvw.sem, 16)

            with sp.Fori(0, B - 1) as turn:
                save((MERGED, turn), False)

            def load_skew(row, qt):
                turn, factor, first = row
                for a in range(4):
                    src = bass.AP(scratch.tensor, scratch.offset + turn * (factor * NT * QS) + ((first * NT + qt) * QS + 32 * a * (ROW + 1) + QL - 1),
                                  [[ROW, 32], [QP, H], [1, QW]])
                    sp.dma_start(skew[32 * a:32 * a + 32, qt % 2, :, 32 * a:32 * a + QW], src).then_inc(s_sk[qt % 2].sem, 16)

            def load_tile(row, t):
                turn, factor, first = row
                at = bass.ds(turn * factor + first, 1)
                sp.dma_start(qk[:, :, t * P:(t + 1) * P].bitcast(F32),
                             qk_d[at].rearrange("a p (j n) -> (a p) j n", n=N)[:, :, t * P:(t + 1) * P]).then_inc(s_tile[t].sem, 16)
                sp.dma_start(v[:, t].rearrange("p h d -> p (h d)"),
                             v_d[at].rearrange("a p (t f) -> (a p) t f", t=NT)[:, t, :]).then_inc(s_tile[t].sem, 16)

            def feed(b, last):
                row = head_row(b)
                after = (row[0], row[1], row[2] - 1)
                for qt in (2, 3):
                    sp.wait_ge(s_sc.sem, s_sc.at(b, (qt - 1) * H))
                    hold(sp)
                    if b[0] == HEADS and qt == 3:
                        for k, written in enumerate(s_lw):
                            sp.wait_ge(written, 32 * LAST_SLOT.count(k))
                    load_skew(row, qt)
                if not last:
                    for t in range(NT - 1):
                        sp.wait_ge(s_pv.sem, s_pv.at(b, (t + 2) * H))
                        hold(sp)
                        load_tile(after, t)
                        if t < 2:
                            sp.wait_ge(s_sc.sem, s_sc.at(b, (t + 3) * H))
                            hold(sp)
                            load_skew(after, t)
                    load_tile(after, NT - 1)

            def put(b):
                sp.wait_ge(s_acc.sem, s_acc.at(b, E + 1))
                hold(sp)
                turn, factor, first = ffn_row(b)
                sp.dma_start(out_d[bass.ds(turn * factor + first, 1)].rearrange("a (t p) d -> p (a t) d", p=P),
                             x[:, bass.ds(turn * (factor * NT) + first * NT, NT), :]).then_inc(s_out, 16)

            left_band(sp, 0)
            load_skew(head_row((HEADS, 0)), 0)
            save((LAST, 0), True)
            sp.wait_ge(s_qkvw.sem, s_qkvw.before((LAST, 0)))
            feed((HEADS, 0), False)
            with sp.Fori(0, B - 2) as turn:
                feed((BOTH, turn), False)
                put((BOTH, turn))
            feed((BOTH, B - 2), True)
            put((BOTH, B - 2))
            put((TAIL, 0))
            sp.wait_ge(s_out, 16 * B)

        @block.gpsimd
        def _(pool):
            nc.gpsimd.memset(mhalf[:], -0.5).then_inc(s_cst, 1)
            pool.wait_ge(s_cst, 1)

            def rsqrt(b, l):
                pool.wait_ge(s_ve.sem, s_ve.at(b, l + 1))
                nc.gpsimd.tensor_tensor(rstd[:], ve[:], mhalf[:], ALU.pow).then_inc(s_rstd.sem, 1)

            def fill_band(i, a):
                for edge in out_of_reach(i, a):
                    nc.gpsimd.memset(edge, NEG).then_inc(s_band, 1)

            def low_weights(parts):
                for k in parts:
                    c0, c1 = WUP_PARTS[k]
                    for i, (whole, first, second) in enumerate(((w1, w1_hi, w1_lo), (w3, w3_hi, w3_lo))):
                        pool.wait_ge(s_whi, 2 * k + i + 1)
                        nc.gpsimd.tensor_tensor(second[:, c0:c1], whole[:, c0:c1], first[:, c0:c1].bitcast(F32),
                                                ALU.subtract).then_inc(s_wlo, 1)

            rsqrt((FIRST, 0), 0)
            low_weights(range(len(WUP_PARTS)))
            pool.wait_ge(s_wlo, 2 * len(WUP_PARTS))
            for n in range(NSLOT):
                nc.gpsimd.memset(rl[:, n, :, :, 0:QL], NEG).then_inc(s_edge, 1)
                nc.gpsimd.memset(rl[:, n, :, :, QL + NREL:QP], NEG).then_inc(s_edge, 1)
            rsqrt((FIRST, 0), 1)
            with pool.Fori(0, B - 1) as turn:
                b = (MERGED, turn)
                rsqrt(b, 0)
                rsqrt(b, 1)
            rsqrt((LAST, 0), 0)
            pool.wait_ge(s_y.sem, s_y.before((LAST, 0)))
            for logits in last_rl[2:]:
                nc.gpsimd.memset(logits[:, :, :, 0:QL], NEG).then_inc(s_pad, 1)
                nc.gpsimd.memset(logits[:, :, :, QL + NREL:QP], NEG).then_inc(s_pad, 1)
            left_band(pool, 0)
            pool.wait_ge(s_pad, 6)
            for a in range(4):
                fill_band(0, a)
            pool.wait_ge(s_lw[2], 32 * LAST_SLOT.count(2))
            pool.wait_ge(s_band, sum(len(out_of_reach(0, a)) for a in range(4)))
            nc.gpsimd.memset(sc[:], NEG).then_inc(s_fill, 1)

            def heads(b):
                for n in range(1, NT * H, 2):
                    pool.wait_ge(s_sc.sem, s_sc.at(b, n + 1))
                    scored = scores_of(n)
                    nc.gpsimd.tensor_tensor(scored, scored, smax[:, n % 4:n % 4 + 1].broadcast_to(scored.shape),
                                            ALU.subtract).then_inc(s_low[1].sem, 1)
                    if b[0] == HEADS and n in FILL_AT:
                        if n == FILL_AT[0]:
                            left_band(pool, 1)
                        pool.wait_ge(s_low[1].sem, s_low[1].at(b, (n + 1) // 2))
                        a = FILL_AT.index(n)
                        fill_band(1, a)
                        pool.wait_ge(s_band, sum(len(out_of_reach(i, c)) for i in range(2) for c in range(4 if i == 0 else a + 1)))

            heads((HEADS, 0))
            rsqrt((HEADS, 0), 0)
            with pool.Fori(0, B - 1) as turn:
                heads((BOTH, turn))
                rsqrt((BOTH, turn), 0)

        @block.vector
        def _(dve):
            def tile_statistics(b, l, row, t):
                nc.vector.bn_stats(stats[:, t, :], xt(row, t)).then_inc(s_stats.sem, 1)
                dve.wait_ge(s_stats.sem, s_stats.at(b, l * NT + t + 1))
                hold(dve)
                nc.vector.bn_aggr(mv[:, t, :], stats[:, t, :]).then_inc(s_mv.sem, 1)

            def variances(b, l):
                dve.wait_ge(s_mv.sem, s_mv.at(b, l * NT + NT))
                nc.vector.tensor_scalar(ve[:], mv[:, :, 1], EPS, None, ALU.add).then_inc(s_ve.sem, 1)

            def statistics(b, l, row):
                for t in range(NT):
                    nc.vector.bn_stats(stats[:, t, :], xt(row, t)).then_inc(s_stats.sem, 1)
                dve.wait_ge(s_stats.sem, s_stats.at(b, l * NT + NT))
                hold(dve)
                for t in range(NT):
                    nc.vector.bn_aggr(mv[:, t, :], stats[:, t, :]).then_inc(s_mv.sem, 1)
                variances(b, l)

            def standardize(b, l, row, to):
                dve.wait_ge(s_rstd.sem, s_rstd.at(b, l + 1))
                hold(dve)
                for t in range(NT):
                    nc.vector.tensor_scalar(xn[:, to, t, :], xt(row, t), mv[:, t, 0:1],
                                            rstd[:, t:t + 1], ALU.subtract, ALU.mult).then_inc(s_xn.sem, 1)

            def gating(b, stage):
                def done(n):
                    dve.wait_ge(s_gv.sem, s_gv.at(b, n))

                logits = bank[:, gate_bank(b[0]), 0:NT * E].rearrange("p (t e) -> p t e", e=E)
                other = gp[:].unsqueeze(2).broadcast_to([P, NT, E, E])
                own = gp[:].unsqueeze(3).broadcast_to([P, NT, E, E])
                if stage == 0:
                    dve.wait_ge(s_gate.sem, s_gate.at(b, 1))
                    nc.vector.tensor_reduce(gmax[:], logits, AX, ALU.max).then_inc(s_gl.sem, 1)
                    dve.wait_ge(s_gl.sem, s_gl.at(b, 1))
                    nc.vector.tensor_tensor(gl[:], logits, gmax[:].unsqueeze(2).broadcast_to([P, NT, E]),
                                            ALU.subtract).then_inc(s_gl.sem, 1)
                if stage == 1:
                    dve.wait_ge(s_gp.sem, s_gp.at(b, 1))
                    nc.vector.tensor_tensor(above[:], other, own, ALU.is_gt).then_inc(s_gv.sem, 1)
                    nc.vector.tensor_tensor(level[:], other, own, ALU.is_ge).then_inc(s_gv.sem, 1)
                if stage == 2:
                    done(2)
                    nc.vector.tensor_tensor(level[:], level[:], tri[:].unsqueeze(1).broadcast_to([P, NT, E, E]),
                                            ALU.mult).then_inc(s_gv.sem, 1)
                if stage == 3:
                    done(3)
                    nc.vector.tensor_tensor(above[:], above[:], level[:], ALU.max).then_inc(s_gv.sem, 1)
                if stage == 4:
                    done(4)
                    nc.vector.tensor_reduce(rank[:], above[:], AX, ALU.add).then_inc(s_gv.sem, 1)
                    nc.vector.tensor_reduce(gsum[:], gp[:], AX, ALU.add).then_inc(s_gv.sem, 1)
                if stage == 5:
                    done(6)
                    nc.vector.reciprocal(ginv[:], gsum[:]).then_inc(s_gv.sem, 1)
                    nc.vector.scalar_tensor_tensor(comb[:], rank[:], 1.5, gp[:], ALU.is_lt, ALU.mult).then_inc(s_gv.sem, 1)
                if stage == 6:
                    done(8)
                    nc.vector.scalar_tensor_tensor(comb[:], comb[:], 0.25, ginv[:].unsqueeze(2).broadcast_to([P, NT, E]),
                                                   ALU.mult, ALU.mult).then_inc(s_comb.sem, 1)

            def low_part(b):
                dve.wait_ge(s_xhi.sem, s_xhi.at(b, 1))
                hold(dve)
                dve.wait_ge(s_xnT.sem, s_xnT.at(b, 1))
                nc.vector.tensor_tensor(xlo[:], xnT[:], xhi[:].bitcast(F32), ALU.subtract).then_inc(s_xlo.sem, 1)

            def hidden(b, u):
                xi, c = UNITS[u]
                m = XC[xi][c][1]
                n = u
                dve.wait_ge(s_th.sem, s_th.at(b, n + 1))
                h1, h3 = h_banks(b[0], u)
                nc.vector.scalar_tensor_tensor(hs[0:m, u % 2, :], th[0:m, u % 2, :], 1.0, bank[0:m, h1, :],
                                               ALU.add, ALU.mult).then_inc(s_hs.sem, 1)
                dve.wait_ge(s_hs.sem, s_hs.at(b, n + 1))
                nc.vector.tensor_tensor(gT[0:m, xi % 2, c, :], hs[0:m, u % 2, :], bank[0:m, h3, :],
                                        ALU.mult).then_inc(s_g.sem, 1)

            def gather(b, xi):
                n = xi
                dve.wait_ge(s_y.sem, s_y.at(b, n + 1))
                hold(dve)
                if xi == 1:
                    dve.wait_ge(s_comb.sem, s_comb.at(b, 1))
                    hold(dve)
                if xi:
                    dve.wait_ge(s_acc.sem, s_acc.at(b, n))
                    hold(dve)
                for t in range(NT):
                    w = comb[:, t, xi - 1:xi] if xi else 0.25
                    before = acc[:, t, :] if xi else xt(ffn_row(b), t)
                    after = acc[:, t, :] if xi < E else xt(ffn_row(b), t)
                    ins = nc.vector.scalar_tensor_tensor(after, bank[:, y_bank(b[0], xi), t * D:(t + 1) * D], w, before,
                                                         ALU.mult, ALU.add)
                ins.then_inc(s_acc.sem, 1)

            def unit(b, u):
                xi, c = UNITS[u]
                hidden(b, u)
                if u == 0 and b[0] == MERGED:
                    standardize(b, 0, side_row(b), 1)
                if (u or b[0] != MERGED) and u < GATE_STAGES:
                    gating(b, u)
                if c == 0 and xi >= 2:
                    gather(b, xi - 2)
                if b[0] != TAIL and u == AHEAD[0]:
                    dve.wait_ge(s_x, 16 * (B - 1))
                    statistics(b, 1, row_ahead(b))
                if b[0] != TAIL and u == AHEAD[1]:
                    standardize(b, 1, row_ahead(b), 0)

            def ffn(b):
                low_part(b)
                for u in range(NU):
                    unit(b, u)
                gather(b, E - 1)
                gather(b, E)

            def side(b, k):
                kind, i = SIDE[k]
                if kind == "gate":
                    gating(b, 0)
                if kind == "v":
                    dve.wait_ge(s_qkvw.sem, s_qkvw.before(b))
                    hold(dve)
                    dve.wait_ge(s_w, 16)
                    dve.wait_ge(s_edge, 2 * NSLOT)
                    dve.wait_ge(s_v.sem, s_v.at(b, 1))
                    nc.vector.tensor_tensor(v[:, :, :, 0:HD],
                                            bank[:, side_bank(b[0], k), :].rearrange("p (t h d) -> p t h d", t=NT, h=H),
                                            bv[:].rearrange("p (h d) -> p h d", h=H).unsqueeze(1).broadcast_to([P, NT, H, HD]),
                                            ALU.add).then_inc(s_vb.sem, 1)
                if kind == "piece" and not on_scalar(i):
                    slot_written(dve, b, k)
                    dve.wait_ge(s_r.sem, s_r.at(b, i + 1))
                    nc.vector.tensor_copy(*piece(b, k)).then_inc(s_rl[0].sem, 1)

            def merged(b):
                low_part(b)
                dve.wait_ge(s_acc.sem, s_acc.before(b))
                hold(dve)
                statistics(b, 0, side_row(b))
                for kind, i in ORDER:
                    if kind == "side":
                        side(b, i)
                    if kind == "hidden":
                        unit(b, i)
                    if kind == "split":
                        split(b, i)
                gather(b, E - 1)
                gather(b, E)

            def split(b, i):
                dve.wait_ge(s_hi.sem, s_hi.at(b, i + 1))
                hold(dve)
                dve.wait_ge(s_lo.sem, s_lo.at(b, i + 1))
                keep = part[:, 0:1] if i < NJ else part[:, 3:4]
                nc.vector.scalar_tensor_tensor(qk[:, i, :], hi[:, i % 2, :].bitcast(F32), keep, lo[:, i % 2, :], ALU.mult, ALU.add).then_inc(s_qk.sem, 1)

            def scores(b, n):
                qt, h = divmod(n, H)
                lo_c, hi_c = scores_window(qt)
                dve.wait_ge(s_s.sem, s_s.at(b, n + 1))
                hold(dve)
                if h == 0:
                    dve.wait_ge(s_sk[qt % 2].sem, s_sk[qt % 2].at(b, 64 * (qt // 2 + 1)))
                    hold(dve)
                    if b[0] == HEADS and qt < 2:
                        dve.wait_ge(s_band, sum(len(out_of_reach(i, a)) for i in range(qt + 1) for a in range(4)))
                if n >= 4:
                    dve.wait_ge(s_t.sem, s_t.at(b, n - 3))
                    hold(dve)
                nc.vector.tensor_tensor_reduce(sc[:, n % 4, OFF + lo_c:OFF + hi_c], bank[:, dot_bank(b[0], n), lo_c:hi_c],
                                               skew[:, qt % 2, h, lo_c:hi_c], 1.0, -3e38, ALU.add, ALU.max,
                                               smax[:, n % 4:n % 4 + 1]).then_inc(s_sc.sem, 1)

            def lower(b, n):
                dve.wait_ge(s_sc.sem, s_sc.at(b, n + 1))
                scored = scores_of(n)
                nc.vector.tensor_scalar(scored, scored, smax[:, n % 4:n % 4 + 1], None, ALU.subtract).then_inc(s_low[n % 2].sem, 1)

            def normalize(b, qt):
                o = bank[:, slot(b[0], "back", qt), :].rearrange("p (h d) -> p h d", h=H)
                dve.wait_ge(s_back.sem, s_back.at(b, qt + 1))
                nc.vector.reciprocal(orec[:], o[:, :, HD]).then_inc(s_orec.sem, 1)
                dve.wait_ge(s_orec.sem, s_orec.at(b, qt + 1))
                nc.vector.tensor_tensor(on[:, qt % 2], o[:, :, 0:HD], orec[:].unsqueeze(2).broadcast_to([P, H, HD]),
                                        ALU.mult).then_inc(s_on.sem, 1)

            def project(b, qt):
                dve.wait_ge(s_xb.sem, s_xb.at(b, NT))
                hold(dve)
                dve.wait_ge(s_y2.sem, s_y2.at(b, qt + 1))
                hold(dve)
                nc.vector.tensor_tensor(xt(head_row(b), qt), bank[:, slot(b[0], "proj", qt), 0:D],
                                        xb[:, qt, :], ALU.add).then_inc(s_x2.sem, 1)

            nc.vector.memset(v[:], 1.0).then_inc(s_fill, 1)
            dve.wait_ge(s_rp, 16)
            dve.wait_ge(s_g0, 16 * 2)
            nc.vector.tensor_copy(rel_hi[:], rel[:]).then_inc(s_rel, 1)
            nc.vector.tensor_scalar(bks[:], bk[:], SCALE, None, ALU.mult).then_inc(s_rel, 1)
            nc.vector.tensor_scalar(bq_lo[:], bq[:], part[:, 2:3], None, ALU.mult).then_inc(s_rel, 1)
            nc.vector.tensor_scalar(bk_lo[:], bk[:], part[:, 5:6], None, ALU.mult).then_inc(s_rel, 1)
            dve.wait_ge(s_rel, 1)
            fl = "p j r -> p (j r)"
            nc.vector.tensor_scalar(rel[:], rel[:], part[:, 4:5], None, ALU.mult).then_inc(s_rel, 1)
            dve.wait_ge(s_rel, 5)
            nc.vector.scalar_tensor_tensor(relr[:].rearrange(fl), rel_hi[:].bitcast(F32).rearrange(fl), part[:, 3:4],
                                           rel[:].rearrange(fl), ALU.mult, ALU.add).then_inc(s_rel, 1)
            nc.vector.memset(x[:, B * NT:(B + 1) * NT, :], 0.0).then_inc(s_fill, 1)
            dve.wait_ge(s_fill, 2)
            dve.wait_ge(s_x0, 16)
            b = (FIRST, 0)
            statistics(b, 0, ffn_row(b))
            standardize(b, 0, ffn_row(b), 0)
            ffn(b)
            with dve.Fori(0, B - 1) as turn:
                merged((MERGED, turn))
            b = (LAST, 0)
            dve.wait_ge(s_acc.sem, s_acc.before(b))
            statistics(b, 0, side_row(b))
            standardize(b, 0, side_row(b), 1)
            for k in range(1, len(SIDE)):
                side(b, k)
                if SIDE[k - 1][0] == "proj":
                    split(b, SIDE[k - 1][1])
            dve.wait_ge(s_fill, 3)
            def heads(b, kind, n):
                if kind == "score":
                    scores(b, n)
                    if n == 4:
                        for t in range(NT):
                            nc.vector.tensor_tensor(xb[:, t, :], xt(head_row(b), t), bp[:], ALU.add).then_inc(s_xb.sem, 1)
                if kind == "low" and n % 2 == 0:
                    lower(b, n)
                if kind == "norm":
                    normalize(b, n)
                if kind == "add":
                    project(b, n)
                if kind == "stat":
                    dve.wait_ge(s_x2.sem, s_x2.at(b, n + 1))
                    hold(dve)
                    tile_statistics(b, 0, head_row(b), n)

            for turn in STEPS[HEADS]:
                for kind, n in turn:
                    heads((HEADS, 0), kind, n)
            variances((HEADS, 0), 0)
            standardize((HEADS, 0), 0, head_row((HEADS, 0)), 0)
            with dve.Fori(0, B - 1) as turn:
                b = (BOTH, turn)
                for kind, i in BOTH_ORDER:
                    if kind == "variances":
                        variances(b, 0)
                    if kind == "standardize":
                        standardize(b, 0, head_row(b), 0)
                    if kind == "low_part":
                        low_part(b)
                    if kind == "gating":
                        gating(b, i)
                    if kind == "hidden":
                        hidden(b, i)
                    if kind == "gather":
                        gather(b, i)
                    if kind in ("heads", "after") and i is not None:
                        for step, n in STEPS[BOTH][i]:
                            if (step in ("score", "low")) == (kind == "heads"):
                                heads(b, step, n)
            ffn((TAIL, 0))

        @block.scalar
        def _(act):
            act.dma_start(small[:], small_d).then_inc(s_g0, 16)
            act.dma_start(rel[:], rel_d).then_inc(s_rp, 16)
            for k, (c0, c1) in enumerate(WUP_PARTS):
                if k < 2:
                    act.wait_ge(*((s_wup, 16 * 2) if k else (s_wsh, 16 * 2)))
                for whole, first in ((w1, w1_hi), (w3, w3_hi)):
                    nc.scalar.copy(first[:, c0:c1], whole[:, c0:c1]).then_inc(s_whi, 1)

            def flip(b):
                act.wait_ge(s_tr.sem, s_tr.at(b, 1))
                nc.scalar.copy(xhi[:], bank[:, flip_bank(b[0]), :]).then_inc(s_xhi.sem, 1)
                nc.scalar.copy(xnT[:], bank[:, flip_bank(b[0]), :]).then_inc(s_xnT.sem, 1)

            def unit(b, u):
                xi, c = UNITS[u]
                m = XC[xi][c][1]
                act.wait_ge(s_h.sem, s_h.at(b, u + 1))
                if u >= 2:
                    act.wait_ge(s_hs.sem, s_hs.at(b, u - 1))
                nc.scalar.activation(th[0:m, u % 2, :], bank[0:m, h_banks(b[0], u)[0], :], ACT.Tanh, scale=0.5).then_inc(s_th.sem, 1)
                if u == 1:
                    act.wait_ge(s_gl.sem, s_gl.at(b, 2))
                    nc.scalar.activation(gp[:], gl[:], ACT.Exp).then_inc(s_gp.sem, 1)

            def ffn(b):
                flip(b)
                for u in range(NU):
                    unit(b, u)

            def side(b, k):
                kind, i = SIDE[k]
                at = bank[:, side_bank(b[0], k), :]
                if kind == "flip":
                    act.wait_ge(s_tr2.sem, s_tr2.at(b, 1))
                    nc.scalar.copy(xnT2[:], at).then_inc(s_xnT2.sem, 1)
                if kind == "proj":
                    scale, bias, scale_lo, bias_lo = (1.0, bq, part[:, 2:3], bq_lo) if i < NJ else (SCALE, bks, part[:, 5:6], bk_lo)
                    j = i % NJ
                    act.wait_ge(s_p.sem, s_p.at(b, i + 1))
                    if i >= 2:
                        act.wait_ge(s_qk.sem, s_qk.at(b, i - 1))
                    nc.scalar.activation(hi[:, i % 2, :], at, ACT.Identity, scale=scale,
                                         bias=bias[:, j:j + 1]).then_inc(s_hi.sem, 1)
                    nc.scalar.activation(lo[:, i % 2, :], at, ACT.Identity, scale=scale_lo,
                                         bias=bias_lo[:, j:j + 1]).then_inc(s_lo.sem, 1)
                if kind == "piece" and on_scalar(i):
                    slot_written(act, b, k)
                    act.wait_ge(s_r.sem, s_r.at(b, i + 1))
                    nc.scalar.copy(*piece(b, k)).then_inc(s_rl[1].sem, 1)

            ffn((FIRST, 0))
            act.wait_ge(s_rel, 4)
            act.wait_ge(s_edge, 2 * NSLOT)
            with act.Fori(0, B - 1) as turn:
                b = (MERGED, turn)
                flip(b)
                for kind, i in ORDER:
                    if kind == "unit":
                        unit(b, i)
                    if kind == "side":
                        side(b, i)
            for k in range(1, len(SIDE)):
                side((LAST, 0), k)
            def heads(b, kind, n):
                if kind == "exp":
                    w = len(QT_CHUNKS[n // H]) * P
                    act.wait_ge(s_t.sem, s_t.at(b, n + 1))
                    if n >= 3:
                        act.wait_ge(s_pv.sem, s_pv.at(b, n - 2))
                    nc.scalar.activation(pT[:, n % 3, 0:w], bank[:, slot(b[0], "turn", n), 0:w], ACT.Exp).then_inc(s_pT.sem, 1)
                if kind == "keep":
                    act.wait_ge(s_pv.sem, s_pv.at(b, (n + 1) * H))
                    if n >= 1:
                        act.wait_ge(s_back.sem, s_back.at(b, n))
                    nc.scalar.copy(oT[:], bank[:, 7, :]).then_inc(s_keep.sem, 1)
                if kind == "oT":
                    act.wait_ge(s_ot.sem, s_ot.at(b, n + 1))
                    if n >= 2:
                        act.wait_ge(s_y2.sem, s_y2.at(b, n - 1))
                    nc.scalar.copy(onT[:, n % 2, :], bank[:, slot(b[0], "oT", n), 0:P]).then_inc(s_onT.sem, 1)

            for turn in STEPS[HEADS]:
                for kind, n in turn:
                    heads((HEADS, 0), kind, n)
            with act.Fori(0, B - 1) as turn:
                b = (BOTH, turn)
                for kind, i in BOTH_ORDER:
                    if kind == "flip":
                        flip(b)
                    if kind == "up" and i[1] == 1:
                        unit(b, i[0])
                    if kind == "heads" and i is not None:
                        for step in STEPS[BOTH][i]:
                            heads(b, *step)
            ffn((TAIL, 0))

        @block.tensor
        def _(pe):
            pe.wait_ge(s_g0, 16 * 2)
            mm = nc.tensor.matmul

            def flip(b):
                for t in range(NT):
                    if b[0] == FIRST:
                        pe.wait_ge(s_xn.sem, s_xn.at(b, t + 1))
                    elif t == 0:
                        pe.wait_ge(s_xn.sem, s_xn.before(b))
                    ins = nc.tensor.transpose(bank[:, flip_bank(b[0]), t * P:(t + 1) * P], xn[:, 0, t, :], ident[:])
                ins.then_inc(s_tr.sem, 1)

            def up(b, u, halves=(0, 1)):
                xi, c = UNITS[u]
                r, m = XC[xi][c]
                cols = slice(WUP_AT[xi] + r, WUP_AT[xi] + r + m)
                if 0 in halves:
                    lag = 2 if b[0] in (MERGED, BOTH) else 3
                    if u >= lag:
                        pe.wait_ge(s_g.sem, s_g.at(b, u - lag + 1))
                    if u == 2 and lag == 3:
                        pe.wait_ge(s_gl.sem, s_gl.at(b, 2))
                    if xi == 0 and c == 0:
                        pe.wait_ge(s_wlo, 2)
                    if xi % 2 and c == 0:
                        pe.wait_ge(s_wlo, xi + 3)
                    if xi == 1 and c == 0:
                        pe.wait_ge(s_wdown, 16 * 5)
                if 1 in halves and b[0] == BOTH and u:
                    pe.wait_ge(s_hs.sem, s_hs.at(b, u))
                for half in halves:
                    at, hi_w, lo_w = h_banks(b[0], u)[half], (w1_hi, w3_hi)[half], (w1_lo, w3_lo)[half]
                    mm(bank[0:m, at, :], hi_w[:, cols], xhi[:], start=True, stop=False)
                    mm(bank[0:m, at, :], lo_w[:, cols], xhi[:], start=False, stop=False)
                    if u == 0 and half == 0:
                        pe.wait_ge(s_xlo.sem, s_xlo.at(b, 1))
                    ins = mm(bank[0:m, at, :], hi_w[:, cols], xlo[:], start=False, stop=True)
                    if half == 1:
                        ins.then_inc(s_h.sem, 1)

            def down(b, xi, tiles):
                if 0 in tiles:
                    pe.wait_ge(s_g.sem, s_g.at(b, sum(len(XC[i]) for i in range(xi + 1))))
                    if b[0] == BOTH:
                        if xi:
                            pe.wait_ge(s_acc.sem, s_acc.at(b, xi))
                        else:
                            pe.wait_ge(s_gl.sem, s_gl.at(b, 2))
                    elif xi >= 2:
                        pe.wait_ge(s_acc.sem, s_acc.at(b, xi - 1))
                    elif xi == 0 and b[0] != FIRST:
                        pe.wait_ge(s_acc.sem, s_acc.before(b))
                for t in tiles:
                    for c, (r, m) in enumerate(XC[xi]):
                        w = w2[0:m, xi - 1, c, :] if xi else sw2[0:m, c, :]
                        ins = mm(bank[:, y_bank(b[0], xi), t * D:(t + 1) * D], gT[0:m, xi % 2, c, t * P:(t + 1) * P], w,
                                 start=(c == 0), stop=(c == len(XC[xi]) - 1))
                if NT - 1 in tiles:
                    ins.then_inc(s_y.sem, 1)

            def gates(b, at):
                pe.wait_ge(s_xnT.sem, s_xnT.at(b, 1))
                if b[0] == BOTH:
                    pe.wait_ge(s_acc.sem, s_acc.before(b))
                for t in range(NT):
                    ins = mm(bank[:, at, t * E:(t + 1) * E], xnT[:, t * P:(t + 1) * P], gate[:], start=True, stop=True)
                ins.then_inc(s_gate.sem, 1)

            def ffn(b):
                flip(b)
                pe.wait_ge(s_xhi.sem, s_xhi.at(b, 1))
                hold(pe)
                for u, (xi, c) in enumerate(UNITS):
                    up(b, u)
                    if u == 0:
                        gates(b, gate_bank(b[0]))
                    if xi and c:
                        down(b, xi - 1, range(2 * c - 2, 2 * c))
                down(b, E, range(NT))

            def side(b, k):
                kind, i = SIDE[k]
                at = side_bank(b[0], k)
                first, ring = (0, 2) if b[0] == MERGED else (1, 8)
                if k - ring >= first:
                    left_bank(pe, b, k - ring)
                if kind == "gate":
                    gates(b, at)
                if kind == "flip":
                    for t in range(NT):
                        pe.wait_ge(s_xn.sem, s_xn.at(b, t + 1))
                        ins = nc.tensor.transpose(bank[:, at, t * P:(t + 1) * P], xn[:, 1, t, :], ident[:])
                    ins.then_inc(s_tr2.sem, 1)
                if kind == "v":
                    pe.wait_ge(s_w, 16)
                    pe.wait_ge(s_xnT2.sem, s_xnT2.at(b, 1))
                    for t in range(NT):
                        ins = mm(bank[:, at, t * D:(t + 1) * D], xnT2[:, t * P:(t + 1) * P], wv[:], start=True, stop=True)
                    ins.then_inc(s_v.sem, 1)
                if kind == "proj":
                    w = (wq if i < NJ else wk)[:, i % NJ, :]
                    mm(bank[:, at, :], w, xnT2[:], start=True, stop=True).then_inc(s_p.sem, 1)
                if kind == "piece":
                    n, g = divmod(i, 4)
                    j, pair = divmod(n, 2)
                    if g == 0:
                        pe.wait_ge(s_rel, 6)
                        pe.wait_ge(s_qk.sem, s_qk.at(b, j + 1))
                    r = slice(32 * g, 32 * g + 32)
                    for row in range(2):
                        q4 = qk[r, j, 2 * pair + row:N:4]
                        ins = mm(bank[:, at, row * RW:(row + 1) * RW], q4, relr[r, j, :], start=True, stop=True)
                    ins.then_inc(s_r.sem, 1)

            def drain(b):
                for k in range(len(SIDE) - (2 if b[0] == MERGED else 8), len(SIDE)):
                    left_bank(pe, b, k)
                    hold(pe)

            ffn((FIRST, 0))
            with pe.Fori(0, B - 1) as turn:
                b = (MERGED, turn)
                flip(b)
                pe.wait_ge(s_xhi.sem, s_xhi.at(b, 1))
                hold(pe)
                for kind, i in ORDER:
                    if kind == "unit":
                        up(b, i)
                    if kind == "side":
                        side(b, i)
                    if kind == "down":
                        xi, half = i
                        down(b, xi, range(2 * half, 2 * half + 2))
                drain(b)
            for k in range(1, len(SIDE)):
                side((LAST, 0), k)
            drain((LAST, 0))

            def free_slot(b, kind, n):
                ring = 1 if b[0] == BOTH else 3
                i = TURNED.index((kind, n))
                if i >= ring:
                    was, m = TURNED[i - ring]
                    read = {"turn": s_pT, "back": s_on, "oT": s_onT, "proj": s_x2}[was]
                    pe.wait_ge(read.sem, read.at(b, m + 1))

            def heads(b, kind, n):
                qt, h = divmod(n, H)
                if kind == "dot":
                    j, g = divmod(h, 4)
                    r = slice(32 * g, 32 * g + 32)
                    lo_c, hi_c = scores_window(qt)
                    k0 = qt * P - (REACH + 1)
                    ring = 2 if b[0] == BOTH else 4
                    if n >= ring:
                        pe.wait_ge(s_sc.sem, s_sc.at(b, n - ring + 1))
                    elif b[0] == BOTH:
                        pe.wait_ge(s_x2.sem, s_x2.before(b))
                    if h == 0:
                        for t in QT_CHUNKS[qt]:
                            pe.wait_ge(s_tile[t].sem, s_tile[t].at(b, 32))
                            hold(pe)
                    ins = mm(bank[:, dot_bank(b[0], n), lo_c:hi_c], qk[r, j, qt * P:(qt + 1) * P], qk[r, NJ + j, k0 + lo_c:k0 + hi_c],
                             start=True, stop=True)
                    ins.then_inc(s_s.sem, 1)
                if kind == "turn":
                    tiles = QT_CHUNKS[qt]
                    first = tiles[0] - qt + 1
                    out = bank[:, slot(b[0], "turn", n), 0:len(tiles) * P]
                    free_slot(b, "turn", n)
                    pe.wait_ge(s_low[n % 2].sem, s_low[n % 2].at(b, n // 2 + 1))
                    for i in range(len(tiles)):
                        ins = nc.tensor.transpose(out[:, i * P:(i + 1) * P], sc[:, n % 4, (first + i) * P:(first + i + 1) * P],
                                                  ident[:])
                    ins.then_inc(s_t.sem, 1)
                if kind == "pv":
                    if h == 0 and qt:
                        pe.wait_ge(s_keep.sem, s_keep.at(b, qt))
                    pe.wait_ge(s_pT.sem, s_pT.at(b, n + 1))
                    tiles = QT_CHUNKS[qt]
                    j, g = divmod(h, 4)
                    for i, kt in enumerate(tiles):
                        ins = mm(bank[32 * g:32 * g + HD + 1, 7, j * P:(j + 1) * P], v[:, kt, h, :],
                                 pT[:, n % 3, i * P:(i + 1) * P], start=(i == 0), stop=(i == len(tiles) - 1))
                    ins.then_inc(s_pv.sem, 1)
                if kind == "back":
                    pe.wait_ge(s_keep.sem, s_keep.at(b, n + 1))
                    free_slot(b, "back", n)
                    for j in range(NJ):
                        ins = nc.tensor.transpose(bank[:, slot(b[0], "back", n), j * P:(j + 1) * P], oT[:, j * P:(j + 1) * P], ident[:])
                    ins.then_inc(s_back.sem, 1)
                if kind == "oT":
                    pe.wait_ge(s_on.sem, s_on.at(b, n + 1))
                    free_slot(b, "oT", n)
                    nc.tensor.transpose(bank[:, slot(b[0], "oT", n), 0:P], on[:, n % 2].rearrange("p h d -> p (h d)"),
                                        ident[:]).then_inc(s_ot.sem, 1)
                if kind == "proj":
                    pe.wait_ge(s_onT.sem, s_onT.at(b, n + 1))
                    free_slot(b, "proj", n)
                    mm(bank[:, slot(b[0], "proj", n), 0:D], onT[:, n % 2, :], wp[:], start=True,
                       stop=True).then_inc(s_y2.sem, 1)

            for turn in STEPS[HEADS]:
                for kind, n in turn:
                    heads((HEADS, 0), kind, n)
            with pe.Fori(0, B - 1) as turn:
                b = (BOTH, turn)
                for kind, i in BOTH_ORDER:
                    if kind == "flip":
                        flip(b)
                    if kind == "up":
                        u, half = i
                        if u == 0 and half == 0:
                            pe.wait_ge(s_xhi.sem, s_xhi.at(b, 1))
                            hold(pe)
                        up(b, u, (half,))
                        if u == 0 and half == 1:
                            gates(b, gate_bank(BOTH))
                    if kind == "down":
                        down(b, i[0], (i[1],))
                    if kind == "heads" and i is not None:
                        for step in STEPS[BOTH][i]:
                            heads(b, *step)
            ffn((TAIL, 0))


_OUTS = [((B, N, D), "float32")]


def kernel(**inputs):
    import numpy as _np
    import concourse.bacc as _bacc
    from concourse import mybir as _mybir
    from concourse.bass_utils import run_bass_kernel_spmd as _run

    a = {k.replace("L0_", ""): _np.asarray(v) for k, v in inputs.items()}

    def copies(w):
        w = w.reshape(NJ, 4, 1, HD, -1)
        return _np.broadcast_to(w, (NJ, 4, 4, HD, w.shape[-1])).reshape(NJ, P, -1)

    wqkv, bqkv = a["attn_qkv_w"].reshape(3, D, D), a["attn_qkv_b"].reshape(3, D)
    rel = _np.zeros((H, HD, RW), _np.float32)
    rel[:, :, :NREL] = a["attn_rel_emb"].transpose(0, 2, 1)
    part = _np.zeros((4, 4, HD, 6), _np.float32)
    for c in range(4):
        for at, low in ((0, c % 2), (3, c // 2)):
            part[:, c, :, at] = -1.0 if low else 1.0
            part[:, c, :, 2 if at == 0 else 4] = 1.0 if low else 0.0
        part[:, c, :, 5] = SCALE * (c // 2)
    arrays = {
        "x": a["attn_x"], "gate": a["ffn_gate_w"].T, "w1": a["ffn_w1"], "w2": a["ffn_w2"], "w3": a["ffn_w3"],
        "sw1": a["ffn_sw1"], "sw2": a["ffn_sw2"], "sw3": a["ffn_sw3"],
        "wq": copies(wqkv[0]).transpose(2, 0, 1), "wk": copies(wqkv[1]).transpose(2, 0, 1), "wv": wqkv[2].T,
        "bq": copies(bqkv[0])[:, :, 0].T, "bk": copies(bqkv[1])[:, :, 0].T, "bv": _np.tile(bqkv[2], (P, 1)),
        "wp": a["attn_proj_w"].T, "bp": _np.tile(a["attn_proj_b"], (P, 1)),
        "rel": copies(rel.reshape(H * HD, RW)).transpose(1, 0, 2),
        "ident": _np.eye(P, dtype=_np.float32), "part": part.reshape(P, 6),
        "tri": _np.broadcast_to(_np.tril(_np.ones((E, E), _np.float32), -1), (P, E, E)),
    }
    arrays["small"] = _np.concatenate([arrays[k].reshape(P, -1) for k in ("gate", "part", "bq", "bk", "tri")], 1)
    arrays["wide"] = _np.concatenate([arrays[k].reshape(P, -1) for k in ("wq", "wk", "wv", "wp", "bv", "bp")], 1)
    nc = _bacc.Bacc("TRN2", target_bir_lowering=False, num_devices=1)
    by_name = {k: _np.ascontiguousarray(arrays[k]) for k in ("x", "w1", "w2", "w3", "sw1", "sw2", "sw3", "small", "wide", "rel", "ident")}
    args = [nc.dram_tensor(f"in_{k}", v.shape, _mybir.dt.from_np(v.dtype), kind="ExternalInput").ap() for k, v in by_name.items()]
    for i, (shape, dtype) in enumerate(_OUTS):
        args.append(nc.dram_tensor(f"out_{i}", shape, _mybir.dt.from_np(_np.dtype(dtype)), kind="ExternalOutput").ap())
    scratch = nc.dram_tensor("scratch", (B * NT * QS,), _mybir.dt.float32, kind="Internal").ap()
    qk = nc.dram_tensor("qk_rows", (B, P, 2 * NJ * N), _mybir.dt.float32, kind="Internal").ap()
    v = nc.dram_tensor("v_rows", (B, P, NT * H * (HD + 1)), _mybir.dt.float32, kind="Internal").ap()
    macaron_kernel(nc, *args, scratch, qk, v)
    r = _run(nc, [{f"in_{k}": v for k, v in by_name.items()}], core_ids=[0])
    return r.results[0]["out_0"]
```
